# Optimizing a Trainium2 kernel written in Bass

```python
import numpy as np
import jax
import jax.numpy as jnp

def _softmax(x, axis=-1):
    return jax.nn.softmax(x, axis=axis)

def _gelu(x):
    return jax.nn.gelu(x, approximate=True)

def _silu(x):
    return jax.nn.silu(x)

def _sigmoid(x):
    return jax.nn.sigmoid(x)

def _layernorm(x, axis=-1, eps=1e-05):
    m = jnp.mean(x, axis=axis, keepdims=True)
    v = jnp.var(x, axis=axis, keepdims=True)
    return (x - m) / jnp.sqrt(v + eps)

def _scatter_add(tgt, idx, src, axis=0):
    return tgt.at[idx].add(src)

def _segment_sum(src, seg, n):
    return jax.ops.segment_sum(src, seg, n)
kernel_name = 'mk_adj_resnorm_d4_adj_r2_1aa055'

def setup_inputs(seed: int=0):
    np.random.seed(seed)
    _w = jnp.asarray

    def _rec_inputs():
        import jax
        import jax.numpy as jnp
        _gk = jax.random.key(seed)
        x = -0.0005207 + 1.001 * jax.random.normal(jax.random.fold_in(_gk, 1), (8, 1024, 128), jnp.float32)
        _a = jax.random.bernoulli(jax.random.fold_in(_gk, 2), 0.00195312, (8, 1024, 1024))
        _a = jnp.logical_or(_a, jnp.swapaxes(_a, -1, -2))
        _a = jnp.logical_or(_a, jnp.eye(1024, dtype=bool))
        _af = _a.astype(jnp.float32)
        _af = _af * jax.random.uniform(jax.random.fold_in(_gk, 3), (8, 1024, 1024), jnp.float32, 0.05, 1)
        adj = _af
        _nm = jnp.ones((8, 1024), dtype=bool)
        nodemask = jnp.where(_nm, 1.0, 0.0).astype(jnp.float32)
        return (x, adj, nodemask)
    x, adj, nodemask = _rec_inputs()

    def _L0_gnn_setup():
        import math
        import jax, jax.numpy as jnp
        import numpy as np
        HIDDEN = 128
        HEADS = 8
        HEAD_DIM = HIDDEN // HEADS
        key = jax.random.key(seed)
        ks = jax.random.split(key, 8)
        b, n = (2, 2048)
        node_state = jax.random.normal(ks[0], (b, n, HIDDEN), dtype=jnp.float32)
        adjacency = jax.random.uniform(ks[1], (b, n, n), dtype=jnp.float32)
        s = 1.0 / math.sqrt(HIDDEN)
        Wq = jax.random.uniform(ks[2], (HIDDEN, HIDDEN), jnp.float32, -s, s)
        Wk = jax.random.uniform(ks[3], (HIDDEN, HIDDEN), jnp.float32, -s, s)
        Wv = jax.random.uniform(ks[4], (HIDDEN, HIDDEN), jnp.float32, -s, s)
        Wo = jax.random.uniform(ks[5], (HIDDEN, HIDDEN), jnp.float32, -s, s)
        bo = jax.random.uniform(ks[6], (HIDDEN,), jnp.float32, -s, s)
        return {'node_state': node_state, 'adjacency': adjacency, 'Wq': Wq, 'Wk': Wk, 'Wv': Wv, 'Wo': Wo, 'bo': bo}
    _L0_gnn_all = _L0_gnn_setup()
    _L0_gnn_in = {k: v for k, v in _L0_gnn_all.items() if k in ('Wq', 'Wk', 'Wv', 'Wo', 'bo')}
    del _L0_gnn_all

    def _L1_gnn_setup():
        import jax, jax.numpy as jnp
        import numpy as np
        B, N, D = (2, 2048, 128)
        key = jax.random.key(seed)
        ks = jax.random.split(key, 6)
        return {'hidden': jax.random.normal(ks[0], (B, N, D), dtype=jnp.float32), 'mask': jax.random.uniform(ks[1], (B, N, N), dtype=jnp.float32), 'W_w': jax.random.normal(ks[2], (D, D), dtype=jnp.float32) * 0.05, 'W_b': jax.random.normal(ks[3], (D,), dtype=jnp.float32) * 0.05, 'a_w': jax.random.normal(ks[4], (2 * D,), dtype=jnp.float32) * 0.05, 'a_b': jax.random.normal(ks[5], (1,), dtype=jnp.float32) * 0.05}
    _L1_gnn_all = _L1_gnn_setup()
    _L1_gnn_in = {k: v for k, v in _L1_gnn_all.items() if k in ('W_w', 'W_b', 'a_w', 'a_b')}
    del _L1_gnn_all

    def _L2_gnn_setup():
        import jax, jax.numpy as jnp
        import numpy as np
        B, N, IN_F, OUT_F = (2, 2048, 128, 128)
        ALPHA = 0.2
        MASK_NEG = -9000000000000000.0
        SINK_NEG = -1000000000.0
        key = jax.random.key(seed)
        kx, kadj, kw, kbw, kai, kbi, kaj, kbj = jax.random.split(key, 8)
        x = jax.random.normal(kx, (B, N, IN_F), dtype=jnp.float32)
        adjs = (jax.random.uniform(kadj, (B, N, N)) < 0.01).astype(jnp.float32)

        def xavier(k, shape, gain=1.414):
            fan_out, fan_in = shape
            bound = gain * np.sqrt(6.0 / (fan_in + fan_out))
            return jax.random.uniform(k, shape, minval=-bound, maxval=bound, dtype=jnp.float32)
        W = xavier(kw, (OUT_F, IN_F))
        bW = jax.random.uniform(kbw, (OUT_F,), minval=-1 / np.sqrt(IN_F), maxval=1 / np.sqrt(IN_F), dtype=jnp.float32)
        wai = xavier(kai, (1, OUT_F))
        bai = jax.random.uniform(kbi, (1,), minval=-1 / np.sqrt(OUT_F), maxval=1 / np.sqrt(OUT_F), dtype=jnp.float32)
        waj = xavier(kaj, (1, OUT_F))
        baj = jax.random.uniform(kbj, (1,), minval=-1 / np.sqrt(OUT_F), maxval=1 / np.sqrt(OUT_F), dtype=jnp.float32)
        return {'x': x, 'adjs': adjs, 'W': W, 'bW': bW, 'wai': wai, 'bai': bai, 'waj': waj, 'baj': baj}
    _L2_gnn_all = _L2_gnn_setup()
    _L2_gnn_in = {k: v for k, v in _L2_gnn_all.items() if k in ('W', 'bW', 'wai', 'bai', 'waj', 'baj')}
    del _L2_gnn_all

    def _L3_gnn_setup():
        import jax, jax.numpy as jnp
        import numpy as np
        EPS = 1e-08
        key = jax.random.key(seed)
        kH, kA, kW = jax.random.split(key, 3)
        B, N, IN, OUT = (32, 256, 128, 128)
        H = jax.random.normal(kH, (B, N, IN), dtype=jnp.float32)
        A = jax.random.uniform(kA, (B, N, N), dtype=jnp.float32)
        mask = jnp.ones((B, N), dtype=jnp.float32)
        W = jax.random.normal(kW, (OUT, IN), dtype=jnp.float32) * (1.0 / np.sqrt(IN))
        b = jnp.zeros((OUT,), dtype=jnp.float32)
        return {'H': H, 'A': A, 'mask': mask, 'W': W, 'b': b}
    _L3_gnn_all = _L3_gnn_setup()
    _L3_gnn_in = {k: v for k, v in _L3_gnn_all.items() if k in ('W', 'b')}
    del _L3_gnn_all
    return {'x': x, 'adj': adj, 'nodemask': nodemask, 'L0_gnn_Wq': _L0_gnn_in['Wq'], 'L0_gnn_Wk': _L0_gnn_in['Wk'], 'L0_gnn_Wv': _L0_gnn_in['Wv'], 'L0_gnn_Wo': _L0_gnn_in['Wo'], 'L0_gnn_bo': _L0_gnn_in['bo'], 'L1_gnn_W_w': _L1_gnn_in['W_w'], 'L1_gnn_W_b': _L1_gnn_in['W_b'], 'L1_gnn_a_w': _L1_gnn_in['a_w'], 'L1_gnn_a_b': _L1_gnn_in['a_b'], 'L2_gnn_W': _L2_gnn_in['W'], 'L2_gnn_bW': _L2_gnn_in['bW'], 'L2_gnn_wai': _L2_gnn_in['wai'], 'L2_gnn_bai': _L2_gnn_in['bai'], 'L2_gnn_waj': _L2_gnn_in['waj'], 'L2_gnn_baj': _L2_gnn_in['baj'], 'L3_gnn_W': _L3_gnn_in['W'], 'L3_gnn_b': _L3_gnn_in['b']}

def reference(x, adj, nodemask, L0_gnn_Wq, L0_gnn_Wk, L0_gnn_Wv, L0_gnn_Wo, L0_gnn_bo, L1_gnn_W_w, L1_gnn_W_b, L1_gnn_a_w, L1_gnn_a_b, L2_gnn_W, L2_gnn_bW, L2_gnn_wai, L2_gnn_bai, L2_gnn_waj, L2_gnn_baj, L3_gnn_W, L3_gnn_b):
    import jax
    import jax.numpy as jnp

    def _L0_gnn_ref(node_state, adjacency, Wq, Wk, Wv, Wo, bo):
        import math
        import jax, jax.numpy as jnp
        import numpy as np
        HIDDEN = 128
        HEADS = 8
        HEAD_DIM = HIDDEN // HEADS
        b, n, _ = node_state.shape

        def split_heads(x):
            return x.reshape(b, n, HEADS, HEAD_DIM).transpose(0, 2, 1, 3)
        q = split_heads(node_state @ Wq.T)
        k = split_heads(node_state @ Wk.T)
        v = split_heads(node_state @ Wv.T)
        scores = jnp.einsum('bhqd,bhkd->bhqk', q, k) / math.sqrt(HEAD_DIM)
        log_adj = jnp.log(adjacency + 1e-06)
        scores = scores + log_adj[:, None, :, :]
        attn = jax.nn.softmax(scores, axis=-1)
        out = jnp.einsum('bhqk,bhkd->bhqd', attn, v)
        out = out.transpose(0, 2, 1, 3).reshape(b, n, HIDDEN)
        return out @ Wo.T + bo

    def _L1_gnn_ref(hidden, mask, W_w, W_b, a_w, a_b):
        import jax, jax.numpy as jnp
        import numpy as np
        B, N, D = (2, 2048, 128)
        h = jnp.einsum('bnd,ed->bne', hidden, W_w) + W_b
        Dh = h.shape[-1]
        a1, a2 = (a_w[:Dh], a_w[Dh:])
        e = h @ a1
        f = h @ a2
        logits = e[:, :, None] + f[:, None, :] + a_b[0]
        u = mask * jnp.exp(logits)
        a = u / jnp.sum(u, axis=2, keepdims=True)
        h_prime = jnp.einsum('bnm,bmd->bnd', a, h)
        return h_prime

    def _L2_gnn_ref(x, adjs, W, bW, wai, bai, waj, baj):
        import jax, jax.numpy as jnp
        import numpy as np
        B, N, IN_F, OUT_F = (2, 2048, 128, 128)
        ALPHA = 0.2
        MASK_NEG = -9000000000000000.0
        SINK_NEG = -1000000000.0
        b, n, _ = adjs.shape
        z = jnp.einsum('bni,oi->bno', x, W) + bW
        ai = jnp.einsum('bno,ko->bnk', z, wai) + bai
        aj = jnp.einsum('bno,ko->bnk', z, waj) + baj
        e = ai + jnp.swapaxes(aj, 1, 2)
        e = jnp.where(e >= 0, e, ALPHA * e)
        att = jnp.where(adjs > 0, e, MASK_NEG)
        sink = jnp.full((b, n, 1), SINK_NEG, dtype=att.dtype)
        att = jax.nn.softmax(jnp.concatenate([att, sink], axis=-1), axis=-1)[:, :, :n]
        return jnp.einsum('bnm,bmo->bno', att, z)

    def _L3_gnn_ref(H, A, mask, W, b):
        import jax, jax.numpy as jnp
        import numpy as np
        EPS = 1e-08
        N = A.shape[-1]
        A_hat = A + jnp.eye(N, dtype=A.dtype)
        deg = A_hat.sum(axis=-1)
        dis = (deg + EPS) ** (-0.5)
        A_norm = dis[:, :, None] * A_hat * dis[:, None, :]
        H_lin = jnp.einsum('bni,oi->bno', H, W) + b
        out = jnp.einsum('bnm,bmo->bno', A_norm, H_lin)
        out = out * mask[:, :, None]
        return jax.nn.relu(out)
    x = _layernorm(x + _L0_gnn_ref(x, adj, L0_gnn_Wq, L0_gnn_Wk, L0_gnn_Wv, L0_gnn_Wo, L0_gnn_bo), axis=-1)
    x = _layernorm(x + _L1_gnn_ref(x, adj, L1_gnn_W_w, L1_gnn_W_b, L1_gnn_a_w, L1_gnn_a_b), axis=-1)
    x = _layernorm(x + _L2_gnn_ref(x, adj, L2_gnn_W, L2_gnn_bW, L2_gnn_wai, L2_gnn_bai, L2_gnn_waj, L2_gnn_baj), axis=-1)
    x = _layernorm(x + _L3_gnn_ref(x, adj, nodemask, L3_gnn_W, L3_gnn_b), axis=-1)
    return x

_drawn_inputs = setup_inputs


def setup_inputs(seed=0):
    import zlib

    import numpy as np

    out = dict(_drawn_inputs(seed))
    spreads = {'L3_gnn_b': (0.0, 0.1)}
    factors = {}
    for name, (base, spread) in spreads.items():
        noise = np.random.default_rng([zlib.crc32(name.encode()), seed]).standard_normal(out[name].shape)
        drawn = base * np.exp(spread * noise) if base else spread * noise
        out[name] = jnp.asarray(drawn.astype(out[name].dtype))
    for name, factor in factors.items():
        out[name] = (out[name] * factor).astype(out[name].dtype)
    return out
```

```python
from contextlib import ExitStack

import concourse.bass as bass
from concourse import mybir

F32 = mybir.dt.float32
BF16 = mybir.dt.bfloat16
ACT = mybir.ActivationFunctionType
ALU = mybir.AluOpType
AX = mybir.AxisListType

P = 128
BANK = 512
HEADS = 8
HD = 16
HG = 4
HP = 2
SLOT = 32
NPROD = 6
Q_PART = (0, 0, 1, 1, 0, 2)
K_PART = (0, 1, 0, 1, 2, 0)
MROW = NPROD * HD
STK = MROW + 2
RING = 8
POOL_KT = (0, 2, 3, 5, 7)
LAG = 3
BIG = 9.0e15
SINK = -1.0e9
LN_EPS = 1e-5
ADJ_EPS = 1e-6
DEG_EPS = 1e-8
SLOPE = 0.2
DVE_LINKS = 151


def gnn_stack_kernel(nc, x, adj, nodemask, Wq, Wk, Wv, Wo, bo, W1, b1, a1w, a1b,
                     W2, b2, wai, bai, waj, baj, W3, b3, out):
    B, N, D = x.shape
    NT = N // P
    QH = N // BANK
    GRP = (HEADS // HG) * QH
    QT = BANK // P
    UN = NT * (HG // HP)
    assert D == P and N == 1024 and HEADS * HD == D
    DVE_KT = tuple(k for k in range(NT) if k not in POOL_KT)
    nD, nP = len(DVE_KT) * (HG // HP), len(POOL_KT) * (HG // HP)
    MAXB = HG * QT * (N // BANK)

    x_v = x.rearrange("b (t p) d -> b p t d", p=P)
    out_v = out.rearrange("b (t p) d -> b p t d", p=P)
    adj_v = adj.rearrange("b (t p) m -> b t p m", p=P)
    qk_dram = nc.dram_tensor("qk_parts", [2, P, 3, N], BF16, kind="Internal").ap()

    with ExitStack() as ctx:
        def sb(name, shape, dt=F32):
            return ctx.enter_context(nc.sbuf_tensor(name, shape, dt))

        def psum(name, shape):
            return ctx.enter_context(nc.psum_tensor(name, shape, F32))

        def sem(name):
            return ctx.enter_context(nc.semaphore(name))

        psS = psum("psS", [P, 2, 2, BANK])
        psO = psum("psO", [P, BANK])
        psX = psum("psX", [P, 2, BANK])
        psM = psum("psM", [P, BANK])
        psS_t = [psS[:, i].rearrange("p a (t c) -> p (a t) c", c=P) for i in range(2)]
        psS_f = [psS[:, i].rearrange("p a c -> p (a c)") for i in range(2)]
        psX_t = psX[:, :, :].rearrange("p a (t c) -> p (a t) c", c=P)
        psX_f = psX[:, :, :].rearrange("p a c -> p (a c)")
        mm_bank = [psX[:, 0], psX[:, 1], psO[:, :], psM[:, :]]

        a_nat = sb("a_nat", [P, NT, N])
        a_t = sb("a_t", [P, NT, N])
        a_te = sb("a_te", [P, len(POOL_KT), N])
        pen = sb("pen", [P, NT, N], BF16)
        qs = sb("qs", [STK, HEADS, N], BF16)
        ks = sb("ks", [STK, HEADS, N], BF16)
        ring = sb("ring", [P, RING, 2 * BANK])
        x_in = sb("x_in", [P, NT, D])
        xc = sb("xc", [P, NT, D])
        y = sb("y", [P, NT, D])
        x_t = sb("x_t", [P, N])
        vaug = sb("vaug", [P, NT, HEADS, SLOT])
        g = sb("g", [P, NT, D + 2])
        o_t = sb("o_t", [P, BANK])
        ident = sb("ident", [P, P])
        identb = sb("identb", [P, P], BF16)
        w_t = sb("w_t", [P, 7, D])
        u12 = sb("u12", [P, 2, 2])
        vrow = sb("vrow", [6, D])
        vcol = sb("vcol", [P, 6])
        brow = sb("brow", [1, 4, D + 2])
        bias = sb("bias", [P, 4, D + 2])
        mask_r = sb("mask_r", [B * NT, P])
        mask = sb("mask", [P, B * NT])
        ones = sb("ones", [1, P])
        rmax = sb("rmax", [P, HG, QT, 2])
        mrow = sb("mrow", [P, HG * QT])
        mpart = sb("mpart", [P, HG * QT, 2], BF16)
        rden = sb("rden", [P, QT, HG])
        st = sb("st", [P, NT, 6])
        mv = sb("mv", [P, NT, 2])
        var = sb("var", [P, NT])
        rstd = sb("rstd", [P, NT])
        mhalf = sb("mhalf", [P, NT])
        ext = sb("ext", [P, NT, 2])
        eexp = sb("eexp", [P, NT, 2])
        deg = sb("deg", [P, NT])
        dis = sb("dis", [P, NT])
        cm = sb("cm", [P, NT])
        sm = sb("sm", [P, 8, NT])
        w12 = sb("w12", [P, 2, NT])
        w_raw = ring[:, 0:1, 0:7 * D].rearrange("p a (w d) -> p (a w) d", d=D)
        on = ring[:, 0, :].rearrange("p (t c) -> p t c", c=D)
        on_t = ring[:, 1, :]
        qkp = [ring[:, 2 + 2 * i:4 + 2 * i, :].bitcast(BF16).rearrange("p a n -> p (a n)")[:, 0:3 * N]
               .rearrange("p (k n) -> p k n", n=N) for i in range(2)]
        res = [ring[:, 6 + i, :] for i in range(2)]

        S = {n: sem(n) for n in (
            "d_w d_small d_xin d_parts d_stack d_out c_const c_wt_ps c_wt c_v_ps c_v c_u_ps c_u c_mask_ps c_row c_bias_ps c_bias "
            "xt_ps xt qk_ps v_ps z1 resid z2 z3 v_sb at_ps at pen ate mx_ps mx mpart mrow_ps mrow "
            "s_ps p_exp p_dve p_pool pv ot ott_ps on ont_ps ont wo xcur var rstd h_ps ext expf g mm1 mm1_free "
            "z_ps ajrow_ps ajcol w12 wrow_ps t2 t e2 p2 mm2 es h3_ps deg dis mm3 mm3_free acc_free "
            "dve act pool").split()}
        d_a = [sem(f"d_a{t}") for t in range(NT)]

        block = ctx.enter_context(nc.Block())

        @block.sync
        def _(sp):
            for w, src in enumerate((Wq, Wk, Wv, Wo, W1, W2, W3)):
                sp.dma_start(w_raw[:, w, :], src).then_inc(S["d_w"], 16)
            sp.dma_start(vrow[0:2, :], a1w.rearrange("(k e) -> k e", k=2)).then_inc(S["d_small"], 16)
            sp.dma_start(vrow[2:3, :], wai).then_inc(S["d_small"], 16)
            sp.dma_start(vrow[3:4, :], waj).then_inc(S["d_small"], 16)
            for i, v in enumerate((b1, b2)):
                sp.dma_start(vrow[4 + i:5 + i, :], v.rearrange("(k e) -> k e", k=1)).then_inc(S["d_small"], 16)
            for i, v in enumerate((bo, b1, b2, b3)):
                sp.dma_start(brow[:, i, 0:D], v.rearrange("(k e) -> k e", k=1)).then_inc(S["d_small"], 16)
            for i, (row, col, v) in enumerate(((1, D, a1b), (2, D, bai), (2, D + 1, baj))):
                sp.dma_start(brow[:, row, col:col + 1], v.rearrange("(k e) -> k e", k=1)).then_inc(S["d_small"], 16)
            sp.dma_start(mask_r[:, :], nodemask.rearrange("b (t p) -> (b t) p", p=P)).then_inc(S["d_small"], 16)
            def load_graph(n):
                sp.dma_start(x_in[:, :, :], x_v[n]).then_inc(S["d_xin"], 16)
                for t in range(NT):
                    sp.dma_start(a_nat[:, t, :], adj_v[n, t]).then_inc(d_a[t], 16)

            def stack_parts(b):
                for i in range(2):
                    sp.wait_ge(S["z3"], b * 2 + i + 1)
                    sp.dma_start(qk_dram[i], qkp[i]).then_inc(S["d_parts"], 16)
                sp.wait_ge(S["d_parts"], b * 32 + 16 * 2)
                for i, (stack, part) in enumerate(((qs, Q_PART), (ks, K_PART))):
                    for j in range(NPROD):
                        src = qk_dram[i, :, part[j], :].rearrange("(h r) n -> r h n", r=HD)
                        sp.dma_start(stack[HD * j:HD * (j + 1), :, :], src).then_inc(S["d_stack"], 16)

            def store_graph(b):
                sp.wait_ge(S["xcur"], b * 4 + 4)
                sp.dma_start(out_v[b], xc[:, :, :]).then_inc(S["d_out"], 16)

            load_graph(0)
            with sp.Fori(0, B - 1) as b:
                stack_parts(b)
                sp.wait_ge(S["at"], b * NT + NT)
                sp.wait_ge(S["pen"], b * NT + NT)
                sp.wait_ge(S["xcur"], b * 4 + 1)
                load_graph(b + 1)
                store_graph(b)
            stack_parts(B - 1)
            store_graph(B - 1)
            sp.wait_ge(S["d_out"], B * 16 + 16)

        @block.gpsimd
        def _(pool):
            nc.gpsimd.memset(ident[:, :], 0.0).then_inc(S["pool"], 1)
            nc.gpsimd.memset(mhalf[:, :], -0.5).then_inc(S["pool"], 1)
            nc.gpsimd.memset(vaug[:, :, :, :], 0.0).then_inc(S["pool"], 1)
            pool.wait_ge(S["pool"], 3)
            nc.gpsimd.affine_select(out=ident[:, :], in_=ident[:, :], compare_op=ALU.not_equal, fill=1.0,
                                    base=0, pattern=[[-1, P]], channel_multiplier=1).then_inc(S["pool"], 1)
            nc.gpsimd.memset(vaug[:, :, :, HD:HD + 1], 1.0).then_inc(S["c_const"], 1)
            pool.wait_ge(S["pool"], 4)
            nc.gpsimd.tensor_copy(identb[:, :], ident[:, :]).then_inc(S["c_const"], 1)
            POOLK = 4

            with pool.Fori(0, B) as b:
                def inv_sqrt(layer):
                    pool.wait_ge(S["var"], b * 4 + layer + 1)
                    nc.gpsimd.tensor_tensor(rstd[:, :], var[:, :], mhalf[:, :], ALU.pow).then_inc(S["rstd"], 1)

                pool.wait_ge(S["ate"], b + 1)
                for i in range(GRP):
                    qh = i % QH
                    for n, kt in enumerate(POOL_KT):
                        for pr in range(HG // HP):
                            u = i * UN + kt * (HG // HP) + pr
                            tile = ring[:, u % RING, :].rearrange("p (h q) -> p h q", h=HP)
                            e = a_te[:, n, qh * BANK:(qh + 1) * BANK].unsqueeze(1).to_broadcast([P, HP, BANK])
                            pool.wait_ge(S["p_exp"], b * GRP * UN + u + 1)
                            nc.gpsimd.tensor_tensor(tile, tile, e, ALU.mult).then_inc(S["p_pool"], 1)
                inv_sqrt(0)
                inv_sqrt(1)
                pool.wait_ge(S["deg"], b + 1)
                nc.gpsimd.tensor_tensor(dis[:, :], deg[:, :], mhalf[:, :], ALU.pow).then_inc(S["dis"], 1)
                inv_sqrt(2)
                inv_sqrt(3)

        @block.scalar
        def _(act):
            act.wait_ge(S["c_wt_ps"], 1)
            nc.scalar.copy(w_t[:, :, :], psS[:, :, :, :].rearrange("p i a (t c) -> p (i a t) c", c=D)[:, 0:7, :]).then_inc(S["c_wt"], 1)
            act.wait_ge(S["c_v_ps"], 1)
            nc.scalar.copy(vcol[:, :], psO[:, 0:6]).then_inc(S["c_v"], 1)
            act.wait_ge(S["c_u_ps"], 1)
            nc.scalar.copy(u12[:, :, :], psM[:, 0:4].rearrange("p (l k) -> p l k", l=2)).then_inc(S["c_u"], 1)
            act.wait_ge(S["c_bias_ps"], 1)
            nc.scalar.copy(bias[:, 0:3, :], psX[:, 0, 0:3 * (D + 2)].rearrange("p (l c) -> p l c", l=3)).then_inc(S["c_bias"], 1)
            nc.scalar.copy(bias[:, 3, :], psX[:, 1, 0:D + 2]).then_inc(S["c_bias"], 1)
            act.wait_ge(S["c_mask_ps"], 1)
            nc.scalar.copy(mask[:, :], psO[:, 0:B * NT]).then_inc(S["c_bias"], 1)

            with act.Fori(0, B) as b:
                def xt_copy(layer):
                    act.wait_ge(S["xt_ps"], b * 4 + layer + 1)
                    nc.scalar.copy(x_t[:, :], psS_f[0]).then_inc(S["xt"], 1)

                def part_copies(i, src, scale):
                    act.wait_ge(S["qk_ps"], b * 2 + i + 1)
                    nc.scalar.activation(qkp[i][:, 0, :], src, ACT.Copy, scale=scale).then_inc(S["z1"], 1)

                xt_copy(0)
                part_copies(0, psS_f[1], 1.0 / HD ** 0.5)
                part_copies(1, psX_f, 1.0)
                act.wait_ge(S["v_ps"], b + 1)
                nc.scalar.copy(vaug[:, :, :, 0:HD],
                               psS_t[0].rearrange("p t (h d) -> p t h d", d=HD)).then_inc(S["v_sb"], 1)
                for i in range(2):
                    act.wait_ge(S["resid"], b * 2 + i + 1)
                    nc.scalar.copy(qkp[i][:, 1, :], res[i]).then_inc(S["z2"], 1)
                for t in range(NT):
                    act.wait_ge(S["at_ps"], b * NT + t + 1)
                    nc.scalar.copy(a_t[:, :, t * P:(t + 1) * P], psS_t[(t + 1) % 2]).then_inc(S["at"], 1)

                def max_rows(i):
                    gi, qh = i // QH, i % QH
                    act.wait_ge(S["mrow_ps"], b * GRP + i + 1)
                    for j in range(HG):
                        last = nc.scalar.copy(qs[MROW:STK, HG * gi + j, qh * BANK:(qh + 1) * BANK],
                                              psM[SLOT * j:SLOT * j + 2, :])
                    last.then_inc(S["mrow"], 1)

                max_rows(0)
                for i in range(GRP):
                    for s in range(UN):
                        u = i * UN + s
                        act.wait_ge(S["s_ps"], b * GRP * UN + u + 1)
                        if u >= RING:
                            act.wait_ge(S["pv"], b * GRP * NT + (u - RING) // (HG // HP) + 1)
                        nc.scalar.activation(ring[:, u % RING, :], psS_f[u % 2], ACT.Exp).then_inc(S["p_exp"], 1)
                        if s == 2 * LAG + 1 and i > 0:
                            act.wait_ge(S["pv"], b * GRP * NT + i * NT)
                            nc.scalar.copy(o_t[:, :], psO[:, :]).then_inc(S["ot"], 1)
                    if i + 1 < GRP:
                        max_rows(i + 1)
                act.wait_ge(S["pv"], b * GRP * NT + GRP * NT)
                nc.scalar.copy(o_t[:, :], psO[:, :]).then_inc(S["ot"], 1)

                act.wait_ge(S["ont_ps"], b + 1)
                nc.scalar.copy(on_t, psS_f[0]).then_inc(S["ont"], 1)

                xt_copy(1)
                act.wait_ge(S["ext"], b + 1)
                nc.scalar.activation(eexp[:, :, :], ext[:, :, :], ACT.Exp).then_inc(S["expf"], 1)

                xt_copy(2)
                act.wait_ge(S["w12"], b + 1)
                nc.scalar.activation(sm[:, 6, :], sm[:, 5, :], ACT.Exp).then_inc(S["es"], 1)
                act.wait_ge(S["wrow_ps"], b + 1)
                for k in range(NT + 1):
                    if k < NT:
                        nc.scalar.activation(ring[:, k, :], psS_f[1], ACT.Identity,
                                             bias=sm[:, 7, k:k + 1]).then_inc(S["t2"], 1)
                    if k > 0:
                        act.wait_ge(S["t"], b * NT + k)
                        nc.scalar.activation(ring[:, k - 1, :], ring[:, k - 1, :], ACT.Exp).then_inc(S["e2"], 1)
                xt_copy(3)

        @block.vector
        def _(dve):
            nc.vector.memset(ones[:, :], 1.0).then_inc(S["c_const"], 1)
            nc.vector.memset(xc[:, :, :], 0.0).then_inc(S["d_out"], 16)
            nc.vector.memset(ks[MROW:STK, :, :], 1.0).then_inc(S["c_const"], 1)
            dve.wait_ge(S["c_u"], 1)
            dve.wait_ge(S["d_small"], 16 * 13)
            nc.vector.tensor_tensor(brow[:, 1, D:D + 1], brow[:, 1, D:D + 1], psM[0:1, 8:9], ALU.add).then_inc(S["c_row"], 1)
            nc.vector.tensor_copy(brow[:, 1, D + 1:D + 2], psM[0:1, 9:10]).then_inc(S["c_row"], 1)
            nc.vector.tensor_tensor(brow[:, 2, D:D + 2], brow[:, 2, D:D + 2], psM[0:1, 10:12], ALU.add).then_inc(S["c_row"], 1)
            nc.vector.memset(brow[:, 0, D:D + 2], 0.0).then_inc(S["c_row"], 1)
            nc.vector.memset(brow[:, 3, D:D + 2], 0.0).then_inc(S["c_row"], 1)
            nc.vector.memset(g[:, :, D:D + 2], 1.0).then_inc(S["dve"], 1)
            dve.wait_ge(S["dve"], 1)

            with dve.Fori(0, B) as b:
                chain = [0]

                def link(ins, tile=None):
                    chain[0] += 1
                    ins.then_inc(S["dve"], 1)
                    if tile is not None and tile >= 0:
                        aggregate(tile)
                    dve.wait_ge(S["dve"], b * DVE_LINKS + chain[0] + 1)

                def spread(cols, width=D):
                    return cols.unsqueeze(2).to_broadcast([P, cols.shape[1], width])

                def statistics(t):
                    link(nc.vector.bn_stats(st[:, t, :], y[:, t, :]))

                def aggregate(t):
                    nc.vector.bn_aggr(mv[:, t, :], st[:, t, :]).then_inc(S["dve"], 1)
                    chain[0] += 1

                def normalise(layer):
                    nc.vector.memset(rmax[:, 0, 0, 0:1], 0.0)
                    for t in range(0 if layer == 0 else NT - 1, NT):
                        aggregate(t)
                    dve.wait_ge(S["dve"], b * DVE_LINKS + chain[0] + 1)
                    nc.vector.tensor_scalar(var[:, :], mv[:, :, 1], LN_EPS, None, ALU.add).then_inc(S["var"], 1)
                    dve.wait_ge(S["rstd"], b * 4 + layer + 1)
                    if layer == 0:
                        dve.wait_ge(S["d_out"], b * 16 + 16)
                    for t in range(NT):
                        last = nc.vector.tensor_scalar(xc[:, t, :], y[:, t, :], mv[:, t, 0:1], rstd[:, t:t + 1],
                                                       ALU.subtract, ALU.mult)
                    last.then_inc(S["xcur"], 1)
                    dve.wait_ge(S["xcur"], b * 4 + layer + 1)

                for i, (src, scale) in enumerate(((psS_f[1], 1.0 / HD ** 0.5), (psX_f, 1.0))):
                    dve.wait_ge(S["z1"], b * 2 + i + 1)
                    nc.vector.scalar_tensor_tensor(res[i], src, scale, qkp[i][:, 0, :],
                                                   ALU.mult, ALU.subtract).then_inc(S["resid"], 1)
                for i in range(2):
                    dve.wait_ge(S["z2"], b * 2 + i + 1)
                    nc.vector.tensor_tensor(qkp[i][:, 2, :], res[i], qkp[i][:, 1, :], ALU.subtract).then_inc(S["z3"], 1)

                for t in range(NT):
                    dve.wait_ge(d_a[t], b * 16 + 16)
                    nc.vector.tensor_scalar(pen[:, t, :], a_nat[:, t, :], 0.0, -BIG, ALU.is_le, ALU.mult).then_inc(S["pen"], 1)
                dve.wait_ge(S["at"], b * NT + NT)
                for n, kt in enumerate(POOL_KT):
                    last = nc.vector.tensor_scalar(a_te[:, n, :], a_t[:, kt, :], ADJ_EPS, None, ALU.add)
                last.then_inc(S["ate"], 1)

                def max_bank(i, m):
                    dve.wait_ge(S["mx_ps"], b * GRP * MAXB + i * MAXB + m + 1)
                    j, qt, kh = m // (2 * QT), m // 2 % QT, m % 2
                    nc.vector.reduce_max(rmax[:, j, qt, kh:kh + 1], psX[:, m % 2, :], AX.X).then_inc(S["mx"], 1)

                def max_parts(i):
                    dve.wait_ge(S["mx"], b * GRP * MAXB + (i + 1) * MAXB)
                    r = rmax[:, :, :, :].rearrange("p j t k -> p (j t) k")
                    link(nc.vector.tensor_tensor(mrow[:, :], r[:, :, 0], r[:, :, 1], ALU.max))
                    link(nc.vector.tensor_scalar(mpart[:, :, 0], mrow[:, :], -1.0, None, ALU.mult))
                    nc.vector.scalar_tensor_tensor(mpart[:, :, 1], mrow[:, :], -1.0, mpart[:, :, 0],
                                                   ALU.mult, ALU.subtract).then_inc(S["mpart"], 1)

                def attention_out(i):
                    gi, qh = i // QH, i % QH
                    dve.wait_ge(S["ott_ps"], b * GRP + i + 1)
                    v = psM[:, :].rearrange("p (t j c) -> p t j c", t=QT, j=HG)
                    link(nc.vector.reciprocal(rden[:, :, :], v[:, :, :, HD]))
                    o = y[:, qh * QT:(qh + 1) * QT, gi * HG * HD:(gi + 1) * HG * HD].rearrange("p t (j d) -> p t j d", d=HD)
                    nc.vector.tensor_tensor(o, v[:, :, :, 0:HD], rden[:, :, :].unsqueeze(3).to_broadcast([P, QT, HG, HD]),
                                            ALU.mult).then_inc(S["on"], 1)

                for m in range(MAXB):
                    max_bank(0, m)
                max_parts(0)
                for i in range(GRP):
                    qh = i % QH
                    m = 0
                    for s in range(UN):
                        kt = s // (HG // HP)
                        u = i * UN + s
                        for _ in range(3):
                            if i + 1 < GRP and m < MAXB:
                                max_bank(i + 1, m)
                                m += 1
                        if kt in DVE_KT:
                            tile = ring[:, u % RING, :].rearrange("p (h q) -> p h q", h=HP)
                            e = a_t[:, kt, qh * BANK:(qh + 1) * BANK].unsqueeze(1).to_broadcast([P, HP, BANK])
                            dve.wait_ge(S["p_exp"], b * GRP * UN + u + 1)
                            nc.vector.scalar_tensor_tensor(tile, e, ADJ_EPS, tile, ALU.add, ALU.mult).then_inc(S["p_dve"], 1)
                        if s == 9 and i > 0:
                            attention_out(i - 1)
                        if s == 11 and i + 1 < GRP:
                            max_parts(i + 1)
                attention_out(GRP - 1)

                dve.wait_ge(S["wo"], b + 1)
                link(nc.vector.tensor_tensor(y[:, :, :], psS_t[1], x_in[:, :, :], ALU.add))
                link(nc.vector.tensor_tensor(y[:, :, :], y[:, :, :], bias[:, 0:1, 0:D].to_broadcast([P, NT, D]), ALU.add))
                for t in range(NT):
                    statistics(t)
                normalise(0)

                def extras(row):
                    link(nc.vector.tensor_tensor(ext[:, :, :], psM[:, 0:2 * NT].rearrange("p (t k) -> p t k", k=2),
                                                 bias[:, row:row + 1, D:D + 2].to_broadcast([P, NT, 2]), ALU.add))

                def biased(row):
                    link(nc.vector.tensor_tensor(g[:, :, 0:D], psS_t[1],
                                                 bias[:, row:row + 1, 0:D].to_broadcast([P, NT, D]), ALU.add))

                dve.wait_ge(S["h_ps"], b + 1)
                extras(1)
                nc.vector.tensor_copy(sm[:, 0, 0:2], ext[:, 0, :]).then_inc(S["ext"], 1)
                biased(1)
                dve.wait_ge(S["expf"], b + 1)
                nc.vector.tensor_tensor(g[:, :, 0:D], g[:, :, 0:D], spread(eexp[:, :, 1]), ALU.mult)
                nc.vector.tensor_copy(g[:, :, D], eexp[:, :, 1]).then_inc(S["g"], 1)
                for t in range(NT):
                    bank = mm_bank[t % 4]
                    dve.wait_ge(S["mm1"], b * NT + t + 1)
                    link(nc.vector.tensor_tensor(sm[:, 0, t:t + 1], bank[:, D:D + 1], eexp[:, t, 0:1], ALU.mult))
                    link(nc.vector.reciprocal(sm[:, 1, t:t + 1], sm[:, 0, t:t + 1]))
                    link(nc.vector.tensor_tensor(sm[:, 2, t:t + 1], sm[:, 1, t:t + 1], eexp[:, t, 0:1], ALU.mult))
                    nc.vector.tensor_scalar(deg[:, t:t + 1], bank[:, D + 1:D + 2], 1.0, DEG_EPS, ALU.add, ALU.add)
                    if t > 0:
                        aggregate(t - 1)
                    ins = nc.vector.scalar_tensor_tensor(y[:, t, :], bank[:, 0:D], sm[:, 2, t:t + 1], xc[:, t, :], ALU.mult, ALU.add)
                    ins.then_inc(S["mm1_free"], 1)
                    dve.wait_ge(S["mm1_free"], b * NT + t + 1)
                    statistics(t)
                nc.vector.memset(g[:, :, D], 1.0).then_inc(S["deg"], 1)
                normalise(1)

                dve.wait_ge(S["z_ps"], b + 1)
                extras(2)
                nc.vector.tensor_scalar(sm[:, 7, :], ext[:, :, 1], SLOPE, None, ALU.mult).then_inc(S["ajcol"], 1)
                dve.wait_ge(S["ajrow_ps"], b + 1)
                nc.vector.tensor_tensor(g[:, :, 0:D], psS_t[1],
                                        bias[:, 2:3, 0:D].to_broadcast([P, NT, D]), ALU.add).then_inc(S["g"], 1)
                for t in range(NT):
                    ins = nc.vector.tensor_tensor_reduce(out=ring[:, t, :], in0=pen[:, t, :], in1=psX_f, scale=1.0,
                                                         scalar=-3.0e38, op0=ALU.add, op1=ALU.max,
                                                         accum_out=sm[:, 0, t:t + 1])
                link(ins)
                link(nc.vector.tensor_tensor(sm[:, 1, :], sm[:, 0, :], ext[:, :, 0], ALU.add))
                link(nc.vector.scalar_tensor_tensor(sm[:, 2, :], sm[:, 1, :], SLOPE, sm[:, 1, :], ALU.mult, ALU.max))
                link(nc.vector.tensor_scalar(sm[:, 3, :], sm[:, 2, :], SINK, None, ALU.max))
                nc.vector.tensor_tensor(w12[:, 0, :], ext[:, :, 0], sm[:, 3, :], ALU.subtract)
                nc.vector.scalar_tensor_tensor(w12[:, 1, :], ext[:, :, 0], SLOPE, sm[:, 3, :], ALU.mult, ALU.subtract)
                nc.vector.tensor_scalar(sm[:, 5, :], sm[:, 3, :], -1.0, SINK, ALU.mult, ALU.add).then_inc(S["w12"], 1)
                dve.wait_ge(S["wrow_ps"], b + 1)
                for k in range(NT + 1):
                    if k < NT:
                        dve.wait_ge(S["t2"], b * NT + k + 1)
                        nc.vector.scalar_tensor_tensor(ring[:, k, :], psS_f[0], ext[:, k, 1:2], ring[:, k, :],
                                                       ALU.add, ALU.max).then_inc(S["t"], 1)
                    if k > 0:
                        dve.wait_ge(S["e2"], b * NT + k)
                        nc.vector.scalar_tensor_tensor(ring[:, k - 1, :], a_t[:, k - 1, :], 0.0, ring[:, k - 1, :],
                                                       ALU.is_gt, ALU.min).then_inc(S["p2"], 1)
                dve.wait_ge(S["mm2"], b + 1)
                dve.wait_ge(S["es"], b + 1)
                for t in range(NT):
                    acc = mm_bank[t // 3][:, (t % 3) * (D + 1):(t % 3 + 1) * (D + 1)]
                    link(nc.vector.tensor_tensor(sm[:, 0, t:t + 1], acc[:, D:D + 1], sm[:, 6, t:t + 1], ALU.add))
                    link(nc.vector.reciprocal(sm[:, 1, t:t + 1], sm[:, 0, t:t + 1]))
                    link(nc.vector.scalar_tensor_tensor(y[:, t, :], acc[:, 0:D], sm[:, 1, t:t + 1], xc[:, t, :],
                                                        ALU.mult, ALU.add), tile=t - 1)
                    statistics(t)
                normalise(2)

                dve.wait_ge(S["dis"], b + 1)
                mb = mask[:, bass.ts(b, NT)]
                link(nc.vector.tensor_tensor(cm[:, :], dis[:, :], mb, ALU.mult))
                dve.wait_ge(S["h3_ps"], b + 1)
                biased(3)
                nc.vector.tensor_tensor(g[:, :, 0:D], g[:, :, 0:D], spread(dis[:, :]), ALU.mult).then_inc(S["g"], 1)
                dve.wait_ge(S["g"], b * 3 + 3)
                for t in range(NT):
                    bank = mm_bank[t % 4]
                    dve.wait_ge(S["mm3"], b * NT + t + 1)
                    ins = nc.vector.tensor_tensor(y[:, t, :], bank[:, 0:D], g[:, t, 0:D], ALU.add)
                    ins.then_inc(S["mm3_free"], 1)
                    dve.wait_ge(S["mm3_free"], b * NT + t + 1)
                    link(nc.vector.tensor_scalar(y[:, t, :], y[:, t, :], cm[:, t:t + 1], 0.0, ALU.mult, ALU.max))
                    link(nc.vector.tensor_tensor(y[:, t, :], y[:, t, :], xc[:, t, :], ALU.add), tile=t - 1)
                    statistics(t)
                normalise(3)
                assert chain[0] == DVE_LINKS, chain[0]

        @block.tensor
        def _(pe):
            mm = nc.tensor.matmul
            pe.wait_ge(S["c_const"], 4)
            pe.wait_ge(S["d_w"], 16 * 7)
            for w in range(7):
                bank, at = w // 4, w % 4
                last = nc.tensor.transpose(psS[:, bank // 2, bank % 2, at * P:(at + 1) * P], w_raw[:, w, :], ident[:, :])
            last.then_inc(S["c_wt_ps"], 1)
            pe.wait_ge(S["d_small"], 16 * 13)
            nc.tensor.transpose(psO[:, 0:6], vrow[:, :], ident[0:6, 0:6]).then_inc(S["c_v_ps"], 1)
            pe.wait_ge(S["c_v"], 1)
            for l in range(2):
                mm(psM[:, 2 * l:2 * l + 2], w_raw[:, 4 + l, :], vcol[:, 2 * l:2 * l + 2], start=True, stop=True)
                last = mm(psM[0:1, 8 + 2 * l:10 + 2 * l], vcol[:, 4 + l:5 + l], vcol[:, 2 * l:2 * l + 2], start=True, stop=True)
            last.then_inc(S["c_u_ps"], 1)
            nc.tensor.transpose(psO[:, 0:B * NT], mask_r[:, :], ident[0:B * NT, 0:B * NT]).then_inc(S["c_mask_ps"], 1)
            pe.wait_ge(S["c_row"], 5)
            rows = brow[:, :, :].rearrange("p l c -> p (l c)")
            mm(psX[:, 0, 0:3 * (D + 2)], ones[:, :], rows[:, 0:3 * (D + 2)], start=True, stop=True)
            mm(psX[:, 1, 0:D + 2], ones[:, :], rows[:, 3 * (D + 2):4 * (D + 2)], start=True, stop=True).then_inc(S["c_bias_ps"], 1)
            pe.wait_ge(S["c_wt"], 1)
            pe.wait_ge(S["c_bias"], 3)

            with pe.Fori(0, B) as b:
                def transposes(src, dst, done):
                    for t in range(NT):
                        last = nc.tensor.transpose(dst[:, t, :], src[:, t, :], ident[:, :])
                    last.then_inc(done, 1)

                def project(dst, w, done, extra=None):
                    for t in range(NT):
                        xt = x_t[:, t * P:(t + 1) * P]
                        last = mm(dst[:, t, :], xt, w_t[:, w, :], start=True, stop=True)
                        if extra is not None:
                            last = mm(psM[:, 2 * t:2 * t + 2], xt, u12[:, extra, :], start=True, stop=True)
                    last.then_inc(done, 1)

                pe.wait_ge(S["d_xin"], b * 16 + 16)
                transposes(x_in, psS_t[0], S["xt_ps"])
                pe.wait_ge(S["xt"], b * 4 + 1)
                for w, dst in enumerate((psS[:, 1], psX)):
                    for h in range(2):
                        last = mm(dst[:, h, :], w_t[:, w, :], x_t[:, h * BANK:(h + 1) * BANK], start=True, stop=True)
                    last.then_inc(S["qk_ps"], 1)
                project(psS_t[0], 2, S["v_ps"])

                for t in range(NT):
                    pe.wait_ge(d_a[t], b * 16 + 16)
                    if t == 0:
                        pe.wait_ge(S["resid"], b * 2 + 1)
                    elif t == 1:
                        pe.wait_ge(S["v_sb"], b + 1)
                    else:
                        pe.wait_ge(S["at"], b * NT + t - 1)
                    for k in range(NT):
                        last = nc.tensor.transpose(psS_t[(t + 1) % 2][:, k, :], a_nat[:, t, k * P:(k + 1) * P], ident[:, :])
                    last.then_inc(S["at_ps"], 1)

                def max_bank(i, m):
                    gi, qh = i // QH, i % QH
                    j, qt, kh = m // (2 * QT), m // 2 % QT, m % 2
                    h, q0 = HG * gi + j, qh * BANK + qt * P
                    n = i * MAXB + m
                    if n >= 2:
                        pe.wait_ge(S["mx"], b * GRP * MAXB + n - 1)
                    mm(psX[:, m % 2, :], qs[0:MROW, h, q0:q0 + P], ks[0:MROW, h, kh * BANK:(kh + 1) * BANK],
                       start=True, stop=True).then_inc(S["mx_ps"], 1)

                def max_rows(i):
                    pe.wait_ge(S["mpart"], b * GRP + i + 1)
                    if i > 1:
                        pe.wait_ge(S["on"], b * GRP + i - 1)
                    for j in range(HG):
                        for qt in range(QT):
                            last = mm(psM[SLOT * j:SLOT * j + 2, qt * P:(qt + 1) * P], mpart[:, j * QT + qt, :],
                                      identb[:, :], start=(qt == 0), stop=(qt == QT - 1), skip_group_check=True,
                                      tile_position=(0, SLOT * j))
                    last.then_inc(S["mrow_ps"], 1)

                def value_products(v):
                    i, kt = v // NT, v % NT
                    if kt == 0 and i > 0:
                        pe.wait_ge(S["ot"], b * GRP + i)
                    if kt in POOL_KT:
                        pe.wait_ge(S["p_pool"], b * GRP * nP + i * nP + (POOL_KT.index(kt) + 1) * (HG // HP))
                    else:
                        pe.wait_ge(S["p_dve"], b * GRP * nD + i * nD + (DVE_KT.index(kt) + 1) * (HG // HP))
                    for j in range(HG):
                        u = v * (HG // HP) + j // HP
                        last = mm(psO[SLOT * j:SLOT * (j + 1), :], vaug[:, kt, HG * (i // QH) + j, :],
                                  ring[:, u % RING, (j % HP) * BANK:(j % HP + 1) * BANK],
                                  start=(kt == 0), stop=(kt == NT - 1), tile_position=(0, SLOT * j), skip_group_check=True)
                    last.then_inc(S["pv"], 1)

                def output_transposes(i):
                    pe.wait_ge(S["ot"], b * GRP + i + 1)
                    if i + 1 < GRP:
                        pe.wait_ge(S["mrow"], b * GRP + i + 1)
                    for t in range(QT):
                        last = nc.tensor.transpose(psM[:, t * P:(t + 1) * P], o_t[:, t * P:(t + 1) * P], ident[:, :])
                    last.then_inc(S["ott_ps"], 1)

                pe.wait_ge(S["d_stack"], b * 16 * 2 * NPROD + 16 * 2 * NPROD)
                pe.wait_ge(S["resid"], b * 2 + 2)
                for m in range(MAXB):
                    max_bank(0, m)
                pe.wait_ge(S["at"], b * NT + NT)
                max_rows(0)
                for i in range(GRP):
                    gi, qh = i // QH, i % QH
                    pe.wait_ge(S["mrow"], b * GRP + i + 1)
                    m = 0
                    for s in range(UN):
                        u = i * UN + s
                        kt, pr = s // (HG // HP), s % (HG // HP)
                        for _ in range(3):
                            if i + 1 < GRP and m < MAXB:
                                max_bank(i + 1, m)
                                m += 1
                        if u >= 2:
                            pe.wait_ge(S["p_exp"], b * GRP * UN + u - 1)
                        for k in range(HP):
                            h = HG * gi + HP * pr + k
                            last = mm(psS[:, u % 2, k, :], ks[:, h, kt * P:(kt + 1) * P],
                                      qs[:, h, qh * BANK:(qh + 1) * BANK], start=True, stop=True)
                        last.then_inc(S["s_ps"], 1)
                        v = u // (HG // HP) - LAG
                        if pr == 1 and v >= 0:
                            value_products(v)
                        if s == 9 and i > 0:
                            output_transposes(i - 1)
                        if s == 13 and i + 1 < GRP:
                            max_rows(i + 1)
                for v in range(GRP * NT - LAG, GRP * NT):
                    value_products(v)
                output_transposes(GRP - 1)

                pe.wait_ge(S["on"], b * GRP + GRP)
                transposes(y, psS_t[0], S["ont_ps"])
                pe.wait_ge(S["ont"], b + 1)
                for t in range(NT):
                    last = mm(psS_t[1][:, t, :], on_t[:, t * P:(t + 1) * P], w_t[:, 3, :], start=True, stop=True)
                last.then_inc(S["wo"], 1)

                pe.wait_ge(S["xcur"], b * 4 + 1)
                transposes(xc, psS_t[0], S["xt_ps"])
                pe.wait_ge(S["xt"], b * 4 + 2)
                project(psS_t[1], 4, S["h_ps"], extra=0)
                pe.wait_ge(S["g"], b * 3 + 1)
                for t in range(NT):
                    if t >= 4:
                        pe.wait_ge(S["mm1_free"], b * NT + t - 3)
                    for k in range(NT):
                        last = mm(mm_bank[t % 4][:, 0:D + 2], a_t[:, k, t * P:(t + 1) * P], g[:, k, :],
                                  start=(k == 0), stop=(k == NT - 1))
                    last.then_inc(S["mm1"], 1)

                pe.wait_ge(S["xcur"], b * 4 + 2)
                transposes(xc, psS_t[0], S["xt_ps"])
                pe.wait_ge(S["xt"], b * 4 + 3)
                project(psS_t[1], 5, S["z_ps"], extra=1)
                pe.wait_ge(S["ajcol"], b + 1)
                for t in range(NT):
                    last = mm(psX_t[:, t, :], ext[:, t, 1:2].to_broadcast([P, P]), ident[:, :], start=True, stop=True)
                last.then_inc(S["ajrow_ps"], 1)
                pe.wait_ge(S["w12"], b + 1)
                pe.wait_ge(S["g"], b * 3 + 2)
                for k in range(2):
                    for t in range(NT):
                        last = mm(psS_t[k][:, t, :], w12[:, k, t:t + 1].to_broadcast([P, P]), ident[:, :], start=True, stop=True)
                last.then_inc(S["wrow_ps"], 1)
                for k in range(NT):
                    pe.wait_ge(S["p2"], b * NT + k + 1)
                    for t in range(NT):
                        last = mm(mm_bank[t // 3][:, (t % 3) * (D + 1):(t % 3 + 1) * (D + 1)],
                                  ring[:, k, t * P:(t + 1) * P], g[:, k, 0:D + 1],
                                  start=(k == 0 and t % 3 == 0), stop=(k == NT - 1), skip_group_check=True)
                last.then_inc(S["mm2"], 1)

                pe.wait_ge(S["xcur"], b * 4 + 3)
                transposes(xc, psS_t[0], S["xt_ps"])
                pe.wait_ge(S["xt"], b * 4 + 4)
                project(psS_t[1], 6, S["h3_ps"])
                pe.wait_ge(S["g"], b * 3 + 3)
                for t in range(NT):
                    if t >= 4:
                        pe.wait_ge(S["mm3_free"], b * NT + t - 3)
                    for k in range(NT):
                        last = mm(mm_bank[t % 4][:, 0:D], a_t[:, k, t * P:(t + 1) * P], g[:, k, 0:D],
                                  start=(k == 0), stop=(k == NT - 1))
                    last.then_inc(S["mm3"], 1)
                pe.wait_ge(S["mm3_free"], b * NT + NT)


_INS = ['x', 'adj', 'nodemask', 'L0_gnn_Wq', 'L0_gnn_Wk', 'L0_gnn_Wv', 'L0_gnn_Wo', 'L0_gnn_bo',
        'L1_gnn_W_w', 'L1_gnn_W_b', 'L1_gnn_a_w', 'L1_gnn_a_b', 'L2_gnn_W', 'L2_gnn_bW', 'L2_gnn_wai',
        'L2_gnn_bai', 'L2_gnn_waj', 'L2_gnn_baj', 'L3_gnn_W', 'L3_gnn_b']


def kernel(**inputs):
    import numpy as _np
    import concourse.bacc as _bacc
    from concourse import mybir as _mybir
    from concourse.bass_utils import run_bass_kernel_spmd as _run

    nc = _bacc.Bacc("TRN2", target_bir_lowering=False, num_devices=1)
    arrays, args = {}, []
    for name in _INS:
        a = _np.ascontiguousarray(inputs[name])
        arrays[f"in_{name}_dram"] = a
        args.append(nc.dram_tensor(f"in_{name}_dram", a.shape, _mybir.dt.from_np(a.dtype), kind="ExternalInput").ap())
    out = nc.dram_tensor("out_0_dram", inputs['x'].shape, _mybir.dt.from_np(_np.dtype('float32')), kind="ExternalOutput").ap()
    gnn_stack_kernel(nc, *args, out)
    r = _run(nc, [arrays], core_ids=[0])
    return r.results[0]["out_0_dram"]
```

```python
from contextlib import ExitStack

import concourse.bass as bass
from concourse import mybir

F32 = mybir.dt.float32
BF16 = mybir.dt.bfloat16
ACT = mybir.ActivationFunctionType
ALU = mybir.AluOpType
AX = mybir.AxisListType

P = 128
BANK = 512
HEADS = 8
HD = 16
HG = 4
HP = 2
SLOT = 32
NPROD = 6
Q_PART = (0, 0, 1, 1, 0, 2)
K_PART = (0, 1, 0, 1, 2, 0)
MROW = NPROD * HD
STK = MROW + 2
RING = 8
POOL_KT = (0, 2, 3, 5, 7)
AHEAD = 6
LAG = 3
BIG = 9.0e15
SINK = -1.0e9
LN_EPS = 1e-5
ADJ_EPS = 1e-6
DEG_EPS = 1e-8
SLOPE = 0.2
DVE_LINKS = 144


def gnn_stack_kernel(nc, x, adj, nodemask, Wq, Wk, Wv, Wo, bo, W1, b1, a1w, a1b,
                     W2, b2, wai, bai, waj, baj, W3, b3, out):
    B, N, D = x.shape
    NT = N // P
    QH = N // BANK
    GRP = (HEADS // HG) * QH
    QT = BANK // P
    UN = NT * (HG // HP)
    assert D == P and N == 1024 and HEADS * HD == D
    DVE_KT = tuple(k for k in range(NT) if k not in POOL_KT)
    nD, nP = len(DVE_KT) * (HG // HP), len(POOL_KT) * (HG // HP)
    MAXB = HG * QT * (N // BANK)

    x_v = x.rearrange("b (t p) d -> b p t d", p=P)
    out_v = out.rearrange("b (t p) d -> b p t d", p=P)
    adj_v = adj.rearrange("b (t p) m -> b t p m", p=P)
    qk_dram = nc.dram_tensor("qk_parts", [2, P, 3, N], BF16, kind="Internal").ap()

    with ExitStack() as ctx:
        def sb(name, shape, dt=F32):
            return ctx.enter_context(nc.sbuf_tensor(name, shape, dt))

        def psum(name, shape):
            return ctx.enter_context(nc.psum_tensor(name, shape, F32))

        def sem(name):
            return ctx.enter_context(nc.semaphore(name))

        psS = psum("psS", [P, 2, 2, BANK])
        psO = psum("psO", [P, BANK])
        psX = psum("psX", [P, 2, BANK])
        psM = psum("psM", [P, BANK])
        psS_t = [psS[:, i].rearrange("p a (t c) -> p (a t) c", c=P) for i in range(2)]
        psS_f = [psS[:, i].rearrange("p a c -> p (a c)") for i in range(2)]
        psX_t = psX[:, :, :].rearrange("p a (t c) -> p (a t) c", c=P)
        psX_f = psX[:, :, :].rearrange("p a c -> p (a c)")
        mm_bank = [psO[:, :], psM[:, :], psX[:, 0]]
        t_bank = [psS[:, 0, 0], psS[:, 0, 1]]
        p_bank = [psS[:, 1, 0], psS[:, 1, 1]]

        a_nat = sb("a_nat", [P, NT, N])
        a_t = sb("a_t", [P, NT, N])
        a_te = sb("a_te", [P, len(POOL_KT), N])
        pen = sb("pen", [P, NT, N], BF16)
        qs = sb("qs", [STK, HEADS, N], BF16)
        ks = sb("ks", [STK, HEADS, N], BF16)
        ring = sb("ring", [P, RING, 2 * BANK])
        x_in = sb("x_in", [P, NT, D])
        xc = sb("xc", [P, NT, D])
        y = sb("y", [P, NT, D])
        x_t = sb("x_t", [P, N])
        vaug = sb("vaug", [P, NT, HEADS, SLOT])
        g = sb("g", [P, NT, D + 2])
        g2 = sb("g2", [P, NT, D + 2])
        o_t = sb("o_t", [P, BANK])
        ident = sb("ident", [P, P])
        identb = sb("identb", [P, P], BF16)
        w_t = sb("w_t", [P, 4, D])
        w_x = sb("w_x", [P, 3, D + 2])
        vcol = sb("vcol", [P, 6])
        bias = sb("bias", [P, 4, D + 2])
        mask = sb("mask", [P, B * NT])
        ones = sb("ones", [1, P])
        rmax = sb("rmax", [P, HG, QT, 2])
        mrow = sb("mrow", [P, HG * QT])
        mpart = sb("mpart", [P, HG * QT, 2], BF16)
        rden = sb("rden", [P, QT, HG])
        st = sb("st", [P, NT, 6])
        mv = sb("mv", [P, NT, 2])
        var = sb("var", [P, NT])
        rstd = sb("rstd", [P, NT])
        mhalf = sb("mhalf", [P, NT])
        ext = sb("ext", [P, NT, 2])
        eexp = sb("eexp", [P, NT, 2])
        deg = sb("deg", [P, NT])
        dis = sb("dis", [P, NT])
        cm = sb("cm", [P, NT])
        sm = sb("sm", [P, 8, NT])
        w12 = sb("w12", [P, 2, NT])
        y_f = y[:, :, :].rearrange("p t d -> p (t d)")
        brow = y_f[0:1, 0:4 * (D + 2)].rearrange("p (l c) -> p l c", l=4)
        vrow = y_f[0:6, 5 * D:6 * D]
        mask_r = y_f[0:B * NT, 6 * D:7 * D]
        w_raw = ring[:, 0:1, 0:7 * D].rearrange("p a (w d) -> p (a w) d", d=D)
        on_t = ring[:, 1, :]
        qkp = [ring[:, 2 + 2 * i:4 + 2 * i, :].bitcast(BF16).rearrange("p a n -> p (a n)")[:, 0:3 * N]
               .rearrange("p (k n) -> p k n", n=N) for i in range(2)]
        res = [ring[:, 6 + i, :] for i in range(2)]

        S = {n: sem(n) for n in (
            "d_w d_small d_xin d_parts d_stack d_out c_const c_wt_ps c_wt c_v_ps c_v c_u_ps c_u c_mask_ps c_row c_bias_ps c_bias "
            "xt_ps xt x0_ps x0 xb qk_ps v_ps z1 resid z2 z3 v_sb at_ps at pen ate mx_ps mx mpart mrow_ps mrow "
            "s_ps p_exp p_dve p_pool pv ot ott_ps on ont_ps ont wo xcur var rstd h_ps hb ext expf g1 g2 g3 mm1 mm1_free "
            "ajrow_ps ajcol w12 wrow_ps t2 t e2 p2 mm2 es deg dis mm3 mm3_free wo_free "
            "dve act pool").split()}
        d_a = [sem(f"d_a{t}") for t in range(NT)]

        block = ctx.enter_context(nc.Block())

        @block.sync
        def _(sp):
            for w, src in enumerate((Wq, Wk, Wv, Wo, W1, W2, W3)):
                sp.dma_start(w_raw[:, w, :], src).then_inc(S["d_w"], 16)
            sp.dma_start(vrow[0:2, :], a1w.rearrange("(k e) -> k e", k=2)).then_inc(S["d_small"], 16)
            sp.dma_start(vrow[2:3, :], wai).then_inc(S["d_small"], 16)
            sp.dma_start(vrow[3:4, :], waj).then_inc(S["d_small"], 16)
            for i, v in enumerate((b1, b2)):
                sp.dma_start(vrow[4 + i:5 + i, :], v.rearrange("(k e) -> k e", k=1)).then_inc(S["d_small"], 16)
            for i, v in enumerate((bo, b1, b2, b3)):
                sp.dma_start(brow[:, i, 0:D], v.rearrange("(k e) -> k e", k=1)).then_inc(S["d_small"], 16)
            for i, (row, col, v) in enumerate(((1, D, a1b), (2, D, bai), (2, D + 1, baj))):
                sp.dma_start(brow[:, row, col:col + 1], v.rearrange("(k e) -> k e", k=1)).then_inc(S["d_small"], 16)
            sp.dma_start(mask_r[:, :], nodemask.rearrange("b (t p) -> (b t) p", p=P)).then_inc(S["d_small"], 16)
            def load_graph(n):
                sp.dma_start(x_in[:, :, :], x_v[n]).then_inc(S["d_xin"], 16)
                for t in range(NT):
                    sp.dma_start(a_nat[:, t, :], adj_v[n, t]).then_inc(d_a[t], 16)

            def stack_parts(b):
                for i in range(2):
                    sp.wait_ge(S["z3"], b * 2 + i + 1)
                    sp.dma_start(qk_dram[i], qkp[i]).then_inc(S["d_parts"], 16)
                sp.wait_ge(S["d_parts"], b * 32 + 16 * 2)
                for i, (stack, part) in enumerate(((qs, Q_PART), (ks, K_PART))):
                    for j in range(NPROD):
                        src = qk_dram[i, :, part[j], :].rearrange("(h r) n -> r h n", r=HD)
                        sp.dma_start(stack[HD * j:HD * (j + 1), :, :], src).then_inc(S["d_stack"], 16)

            def store_graph(b):
                sp.wait_ge(S["xcur"], b * 4 * NT + 4 * NT)
                sp.dma_start(out_v[b], xc[:, :, :]).then_inc(S["d_out"], 16)

            load_graph(0)
            with sp.Fori(0, B - 1) as b:
                stack_parts(b)
                sp.wait_ge(S["at"], b * NT + NT)
                sp.wait_ge(S["pen"], b * NT + NT)
                sp.wait_ge(S["xcur"], b * 4 * NT + NT)
                load_graph(b + 1)
                store_graph(b)
            stack_parts(B - 1)
            store_graph(B - 1)
            sp.wait_ge(S["d_out"], B * 16 + 16)

        @block.gpsimd
        def _(pool):
            nc.gpsimd.memset(ident[:, :], 0.0).then_inc(S["pool"], 1)
            nc.gpsimd.memset(mhalf[:, :], -0.5).then_inc(S["pool"], 1)
            nc.gpsimd.memset(vaug[:, :, :, :], 0.0).then_inc(S["pool"], 1)
            pool.wait_ge(S["pool"], 3)
            nc.gpsimd.affine_select(out=ident[:, :], in_=ident[:, :], compare_op=ALU.not_equal, fill=1.0,
                                    base=0, pattern=[[-1, P]], channel_multiplier=1).then_inc(S["pool"], 1)
            nc.gpsimd.memset(vaug[:, :, :, HD:HD + 1], 1.0).then_inc(S["c_const"], 1)
            pool.wait_ge(S["pool"], 4)
            nc.gpsimd.tensor_copy(identb[:, :], ident[:, :]).then_inc(S["c_const"], 1)
            pool.wait_ge(S["c_bias"], 3)

            with pool.Fori(0, B) as b:
                def inv_sqrt(layer):
                    for t in range(NT):
                        pool.wait_ge(S["var"], b * 4 * NT + layer * NT + t + 1)
                        nc.gpsimd.tensor_tensor(rstd[:, t:t + 1], var[:, t:t + 1], mhalf[:, t:t + 1],
                                                ALU.pow).then_inc(S["rstd"], 1)

                pool.wait_ge(S["x0_ps"], b + 1)
                nc.gpsimd.tensor_tensor(x_in[:, :, :], x_in[:, :, :], bias[:, 0:1, 0:D].to_broadcast([P, NT, D]),
                                        ALU.add).then_inc(S["xb"], 1)
                pool.wait_ge(S["ate"], b + 1)
                for i in range(GRP):
                    qh = i % QH
                    for n, kt in enumerate(POOL_KT):
                        for pr in range(HG // HP):
                            u = i * UN + kt * (HG // HP) + pr
                            tile = ring[:, u % RING, :].rearrange("p (h q) -> p h q", h=HP)
                            e = a_te[:, n, qh * BANK:(qh + 1) * BANK].unsqueeze(1).to_broadcast([P, HP, BANK])
                            pool.wait_ge(S["p_exp"], b * GRP * UN + u + 1)
                            nc.gpsimd.tensor_tensor(tile, tile, e, ALU.mult).then_inc(S["p_pool"], 1)
                inv_sqrt(0)
                inv_sqrt(1)
                pool.wait_ge(S["deg"], b + 1)
                nc.gpsimd.tensor_tensor(dis[:, :], deg[:, :], mhalf[:, :], ALU.pow).then_inc(S["dis"], 1)
                inv_sqrt(2)
                inv_sqrt(3)

        @block.scalar
        def _(act):
            act.wait_ge(S["c_wt_ps"], 1)
            nc.scalar.copy(w_t[:, :, :], psS[:, 0, 0, :].rearrange("p (t c) -> p t c", c=D)).then_inc(S["c_wt"], 1)
            nc.scalar.copy(w_x[:, :, 0:D], psS[:, 0, 1, :].rearrange("p (t c) -> p t c", c=D)[:, 0:3, :]).then_inc(S["c_wt"], 1)
            act.wait_ge(S["c_v_ps"], 1)
            nc.scalar.copy(vcol[:, :], psO[:, 0:6]).then_inc(S["c_v"], 1)
            act.wait_ge(S["c_u_ps"], 1)
            nc.scalar.copy(w_x[:, 0:2, D:D + 2], psM[:, 0:4].rearrange("p (l k) -> p l k", l=2)).then_inc(S["c_u"], 1)
            act.wait_ge(S["c_bias_ps"], 1)
            nc.scalar.copy(bias[:, 0:3, :], psX[:, 0, 0:3 * (D + 2)].rearrange("p (l c) -> p l c", l=3)).then_inc(S["c_bias"], 1)
            nc.scalar.copy(bias[:, 3, :], psX[:, 1, 0:D + 2]).then_inc(S["c_bias"], 1)
            act.wait_ge(S["c_mask_ps"], 1)
            nc.scalar.copy(mask[:, :], psO[:, 0:B * NT]).then_inc(S["c_bias"], 1)

            with act.Fori(0, B) as b:
                def xt_copy(layer, t):
                    act.wait_ge(S["xt_ps"], b * 3 * NT + (layer - 1) * NT + t + 1)
                    nc.scalar.copy(x_t[:, t * P:(t + 1) * P], t_bank[t % 2][:, 0:P]).then_inc(S["xt"], 1)

                def exp_rows(t):
                    act.wait_ge(S["ext"], b * 2 * NT + t + 1)
                    nc.scalar.activation(eexp[:, t, :], ext[:, t, :], ACT.Exp).then_inc(S["expf"], 1)
                    act.wait_ge(S["expf"], b * NT + t + 1)
                    nc.scalar.copy(g[:, t, D:D + 1], eexp[:, t, 1:2])
                    act.wait_ge(S["hb"], b * 2 * NT + t + 1)
                    nc.scalar.activation(g[:, t, 0:D], g[:, t, 0:D], ACT.Copy, scale=eexp[:, t, 1:2]).then_inc(S["g1"], 1)

                def scale_rows(t):
                    act.wait_ge(S["hb"], b * 2 * NT + NT + t + 1)
                    nc.scalar.activation(g[:, t, 0:D], g[:, t, 0:D], ACT.Copy, scale=dis[:, t:t + 1]).then_inc(S["g3"], 1)

                def part_copies(i, src, scale):
                    act.wait_ge(S["qk_ps"], b * 2 + i + 1)
                    nc.scalar.activation(qkp[i][:, 0, :], src, ACT.Copy, scale=scale).then_inc(S["z1"], 1)

                act.wait_ge(S["x0_ps"], b + 1)
                nc.scalar.copy(x_t[:, :], psS_f[0]).then_inc(S["x0"], 1)
                part_copies(0, psS_f[1], 1.0 / HD ** 0.5)
                part_copies(1, psX_f, 1.0)
                act.wait_ge(S["v_ps"], b + 1)
                nc.scalar.copy(vaug[:, :, :, 0:HD],
                               psS_t[0].rearrange("p t (h d) -> p t h d", d=HD)).then_inc(S["v_sb"], 1)
                for i in range(2):
                    act.wait_ge(S["resid"], b * 2 + i + 1)
                    nc.scalar.copy(qkp[i][:, 1, :], res[i]).then_inc(S["z2"], 1)
                for t in range(NT):
                    act.wait_ge(S["at_ps"], b * NT + t + 1)
                    nc.scalar.copy(a_t[:, :, t * P:(t + 1) * P], psS_t[(t + 1) % 2]).then_inc(S["at"], 1)

                def max_rows(i):
                    gi, qh = i // QH, i % QH
                    act.wait_ge(S["mrow_ps"], b * GRP + i + 1)
                    for j in range(HG):
                        last = nc.scalar.copy(qs[MROW:STK, HG * gi + j, qh * BANK:(qh + 1) * BANK],
                                              psM[SLOT * j:SLOT * j + 2, :])
                    last.then_inc(S["mrow"], 1)

                max_rows(0)
                for i in range(GRP):
                    for s in range(UN):
                        u = i * UN + s
                        act.wait_ge(S["s_ps"], b * GRP * UN + u + 1)
                        if u >= RING:
                            act.wait_ge(S["pv"], b * GRP * NT + (u - RING) // (HG // HP) + 1)
                        nc.scalar.activation(ring[:, u % RING, :], psS_f[u % 2], ACT.Exp).then_inc(S["p_exp"], 1)
                        if s == 2 * LAG + 1 and i > 0:
                            act.wait_ge(S["pv"], b * GRP * NT + i * NT)
                            nc.scalar.copy(o_t[:, :], psO[:, :]).then_inc(S["ot"], 1)
                    if i + 1 < GRP:
                        max_rows(i + 1)
                act.wait_ge(S["pv"], b * GRP * NT + GRP * NT)
                nc.scalar.copy(o_t[:, :], psO[:, :]).then_inc(S["ot"], 1)

                for s in range(NT + 4):
                    if s < NT:
                        act.wait_ge(S["ont_ps"], b * NT + s + 1)
                        nc.scalar.copy(on_t[:, s * P:(s + 1) * P], psX[:, s % 2, 0:P]).then_inc(S["ont"], 1)
                    if 0 <= s - 3 < NT:
                        xt_copy(1, s - 3)
                    if s >= 4:
                        exp_rows(s - 4)
                for t in range(NT):
                    xt_copy(2, t)
                act.wait_ge(S["w12"], b + 1)
                nc.scalar.activation(sm[:, 6, :], sm[:, 5, :], ACT.Exp).then_inc(S["es"], 1)
                act.wait_ge(S["wrow_ps"], b + 1)
                for k in range(NT + 1):
                    if k < NT:
                        nc.scalar.activation(ring[:, k, :], psS_f[1], ACT.Identity,
                                             bias=sm[:, 7, k:k + 1]).then_inc(S["t2"], 1)
                    if k > 0:
                        act.wait_ge(S["t"], b * NT + k)
                        nc.scalar.activation(ring[:, k - 1, :], ring[:, k - 1, :], ACT.Exp).then_inc(S["e2"], 1)
                act.wait_ge(S["dis"], b + 1)
                for s in range(NT + 3):
                    if s < NT:
                        xt_copy(3, s)
                    if s >= 3:
                        scale_rows(s - 3)

        @block.vector
        def _(dve):
            nc.vector.memset(ones[:, :], 1.0).then_inc(S["c_const"], 1)
            nc.vector.memset(xc[:, :, :], 0.0).then_inc(S["d_out"], 16)
            nc.vector.memset(ks[MROW:STK, :, :], 1.0).then_inc(S["c_const"], 1)
            dve.wait_ge(S["c_u"], 1)
            dve.wait_ge(S["d_small"], 16 * 13)
            nc.vector.tensor_tensor(brow[:, 1, D:D + 1], brow[:, 1, D:D + 1], psM[0:1, 8:9], ALU.add).then_inc(S["c_row"], 1)
            nc.vector.tensor_copy(brow[:, 1, D + 1:D + 2], psM[0:1, 9:10]).then_inc(S["c_row"], 1)
            nc.vector.tensor_tensor(brow[:, 2, D:D + 2], brow[:, 2, D:D + 2], psM[0:1, 10:12], ALU.add).then_inc(S["c_row"], 1)
            nc.vector.memset(brow[:, 0, D:D + 2], 0.0).then_inc(S["c_row"], 1)
            nc.vector.memset(brow[:, 3, D:D + 2], 0.0).then_inc(S["c_row"], 1)
            nc.vector.memset(g[:, :, D + 1], 1.0).then_inc(S["dve"], 1)
            nc.vector.memset(g2[:, :, D], 1.0).then_inc(S["dve"], 1)
            dve.wait_ge(S["dve"], 2)

            with dve.Fori(0, B) as b:
                chain = [0]

                def link(ins):
                    chain[0] += 1
                    ins.then_inc(S["dve"], 1)
                    dve.wait_ge(S["dve"], b * DVE_LINKS + chain[0] + 2)

                def apply_norm(layer, t):
                    if layer == 0 and t == 0:
                        dve.wait_ge(S["d_out"], b * 16 + 16)
                    dve.wait_ge(S["rstd"], b * 4 * NT + layer * NT + t + 1)
                    nc.vector.tensor_scalar(xc[:, t, :], y[:, t, :], mv[:, t, 0:1], rstd[:, t:t + 1],
                                            ALU.subtract, ALU.mult).then_inc(S["xcur"], 1)

                def normalise(layer, t):
                    link(nc.vector.bn_stats(st[:, t, :], y[:, t, :]))
                    if t > 0:
                        apply_norm(layer, t - 1)
                    else:
                        nc.vector.memset(rmax[:, 0, 0, 0:1], 0.0)
                    link(nc.vector.bn_aggr(mv[:, t, :], st[:, t, :]))
                    nc.vector.tensor_scalar(var[:, t:t + 1], mv[:, t, 1:2], LN_EPS, None, ALU.add).then_inc(S["var"], 1)

                def biased(layer, t, dst):
                    bank = p_bank[t % 2]
                    dve.wait_ge(S["h_ps"], b * 3 * NT + (layer - 1) * NT + t + 1)
                    if layer < 3:
                        nc.vector.tensor_tensor(ext[:, t, :], bank[:, D:D + 2], bias[:, layer, D:D + 2],
                                                ALU.add).then_inc(S["ext"], 1)
                    nc.vector.tensor_tensor(dst[:, t, 0:D], bank[:, 0:D], bias[:, layer, 0:D],
                                            ALU.add).then_inc(S["g2" if layer == 2 else "hb"], 1)

                for i, (src, scale) in enumerate(((psS_f[1], 1.0 / HD ** 0.5), (psX_f, 1.0))):
                    dve.wait_ge(S["z1"], b * 2 + i + 1)
                    nc.vector.scalar_tensor_tensor(res[i], src, scale, qkp[i][:, 0, :],
                                                   ALU.mult, ALU.subtract).then_inc(S["resid"], 1)
                for i in range(2):
                    dve.wait_ge(S["z2"], b * 2 + i + 1)
                    nc.vector.tensor_tensor(qkp[i][:, 2, :], res[i], qkp[i][:, 1, :], ALU.subtract).then_inc(S["z3"], 1)

                for t in range(NT):
                    dve.wait_ge(d_a[t], b * 16 + 16)
                    nc.vector.tensor_scalar(pen[:, t, :], a_nat[:, t, :], 0.0, -BIG, ALU.is_le, ALU.mult).then_inc(S["pen"], 1)
                dve.wait_ge(S["at"], b * NT + NT)
                for n, kt in enumerate(POOL_KT):
                    last = nc.vector.tensor_scalar(a_te[:, n, :], a_t[:, kt, :], ADJ_EPS, None, ALU.add)
                last.then_inc(S["ate"], 1)

                def max_bank(n):
                    m = n % MAXB
                    j, qt, kh = m // (2 * QT), m // 2 % QT, m % 2
                    dve.wait_ge(S["mx_ps"], b * GRP * MAXB + n + 1)
                    nc.vector.reduce_max(rmax[:, j, qt, kh:kh + 1], psX[:, n % 2, :], AX.X).then_inc(S["mx"], 1)

                def max_parts(i):
                    dve.wait_ge(S["mx"], b * GRP * MAXB + (i + 1) * MAXB)
                    r = rmax[:, :, :, :].rearrange("p j t k -> p (j t) k")
                    link(nc.vector.tensor_tensor(mrow[:, :], r[:, :, 0], r[:, :, 1], ALU.max))
                    link(nc.vector.tensor_scalar(mpart[:, :, 0], mrow[:, :], -1.0, None, ALU.mult))
                    nc.vector.scalar_tensor_tensor(mpart[:, :, 1], mrow[:, :], -1.0, mpart[:, :, 0],
                                                   ALU.mult, ALU.subtract).then_inc(S["mpart"], 1)

                def attention_out(i):
                    gi, qh = i // QH, i % QH
                    dve.wait_ge(S["ott_ps"], b * GRP + i + 1)
                    v = psM[:, :].rearrange("p (t j c) -> p t j c", t=QT, j=HG)
                    link(nc.vector.reciprocal(rden[:, :, :], v[:, :, :, HD]))
                    o = y[:, qh * QT:(qh + 1) * QT, gi * HG * HD:(gi + 1) * HG * HD].rearrange("p t (j d) -> p t j d", d=HD)
                    nc.vector.tensor_tensor(o, v[:, :, :, 0:HD], rden[:, :, :].unsqueeze(3).to_broadcast([P, QT, HG, HD]),
                                            ALU.mult).then_inc(S["on"], 1)

                def weigh(u):
                    i, kt = u // UN, u % UN // (HG // HP)
                    if kt in DVE_KT:
                        qh = i % QH
                        tile = ring[:, u % RING, :].rearrange("p (h q) -> p h q", h=HP)
                        e = a_t[:, kt, qh * BANK:(qh + 1) * BANK].unsqueeze(1).to_broadcast([P, HP, BANK])
                        dve.wait_ge(S["p_exp"], b * GRP * UN + u + 1)
                        nc.vector.scalar_tensor_tensor(tile, e, ADJ_EPS, tile, ALU.add, ALU.mult).then_inc(S["p_dve"], 1)

                n = 0
                for n in range(MAXB + AHEAD):
                    max_bank(n)
                    if (n + 1) % MAXB == 0:
                        max_parts(n // MAXB)
                for u in range(GRP * UN):
                    for n in range(MAXB + AHEAD + 2 * u, min(MAXB + AHEAD + 2 * u + 2, GRP * MAXB)):
                        max_bank(n)
                        if (n + 1) % MAXB == 0:
                            max_parts(n // MAXB)
                    if u >= 2:
                        weigh(u - 2)
                    if u % UN == 9 and u > UN:
                        attention_out(u // UN - 1)
                weigh(GRP * UN - 2)
                weigh(GRP * UN - 1)
                attention_out(GRP - 1)

                dve.wait_ge(S["xb"], b + 1)
                for t in range(NT):
                    dve.wait_ge(S["wo"], b * NT + t + 1)
                    ins = nc.vector.tensor_tensor(y[:, t, :], mm_bank[t % 2][:, 0:D], x_in[:, t, :], ALU.add)
                    ins.then_inc(S["wo_free"], 1)
                    dve.wait_ge(S["wo_free"], b * NT + t + 1)
                    normalise(0, t)
                    if t >= 3:
                        biased(1, t - 3, g)
                apply_norm(0, NT - 1)
                for t in range(NT - 3, NT):
                    biased(1, t, g)

                dve.wait_ge(S["expf"], b * NT + NT)
                for t in range(NT):
                    bank = mm_bank[t % 2]
                    dve.wait_ge(S["mm1"], b * NT + t + 1)
                    link(nc.vector.tensor_tensor(sm[:, 0, t:t + 1], bank[:, D:D + 1], eexp[:, t, 0:1], ALU.mult))
                    link(nc.vector.reciprocal(sm[:, 1, t:t + 1], sm[:, 0, t:t + 1]))
                    link(nc.vector.tensor_tensor(sm[:, 2, t:t + 1], sm[:, 1, t:t + 1], eexp[:, t, 0:1], ALU.mult))
                    ins = nc.vector.tensor_scalar(deg[:, t:t + 1], bank[:, D + 1:D + 2], 1.0, DEG_EPS, ALU.add, ALU.add)
                    if t == NT - 1:
                        ins.then_inc(S["deg"], 1)
                    ins = nc.vector.scalar_tensor_tensor(y[:, t, :], bank[:, 0:D], sm[:, 2, t:t + 1], xc[:, t, :], ALU.mult, ALU.add)
                    ins.then_inc(S["mm1_free"], 1)
                    dve.wait_ge(S["mm1_free"], b * NT + t + 1)
                    normalise(1, t)
                    if t >= 3:
                        biased(2, t - 3, g2)
                apply_norm(1, NT - 1)
                for t in range(NT - 3, NT):
                    biased(2, t, g2)

                dve.wait_ge(S["ext"], b * 2 * NT + 2 * NT)
                nc.vector.tensor_scalar(sm[:, 7, :], ext[:, :, 1], SLOPE, None, ALU.mult)
                dve.wait_ge(S["ajrow_ps"], b + 1)
                nc.vector.memset(rmax[:, 0, 0, 0:1], 0.0)
                for t in range(NT):
                    ins = nc.vector.tensor_tensor_reduce(out=ring[:, t, :], in0=pen[:, t, :], in1=psX_f, scale=1.0,
                                                         scalar=-3.0e38, op0=ALU.add, op1=ALU.max,
                                                         accum_out=sm[:, 0, t:t + 1])
                link(ins)
                link(nc.vector.tensor_tensor(sm[:, 1, :], sm[:, 0, :], ext[:, :, 0], ALU.add))
                link(nc.vector.scalar_tensor_tensor(sm[:, 2, :], sm[:, 1, :], SLOPE, sm[:, 1, :], ALU.mult, ALU.max))
                link(nc.vector.tensor_scalar(sm[:, 3, :], sm[:, 2, :], SINK, None, ALU.max))
                nc.vector.tensor_tensor(w12[:, 0, :], ext[:, :, 0], sm[:, 3, :], ALU.subtract)
                nc.vector.scalar_tensor_tensor(w12[:, 1, :], ext[:, :, 0], SLOPE, sm[:, 3, :], ALU.mult, ALU.subtract)
                nc.vector.tensor_scalar(sm[:, 5, :], sm[:, 3, :], -1.0, SINK, ALU.mult, ALU.add).then_inc(S["w12"], 1)
                dve.wait_ge(S["wrow_ps"], b + 1)
                for k in range(NT + 1):
                    if k < NT:
                        dve.wait_ge(S["t2"], b * NT + k + 1)
                        nc.vector.scalar_tensor_tensor(ring[:, k, :], psS_f[0], ext[:, k, 1:2], ring[:, k, :],
                                                       ALU.add, ALU.max).then_inc(S["t"], 1)
                    if k > 0:
                        dve.wait_ge(S["e2"], b * NT + k)
                        nc.vector.scalar_tensor_tensor(ring[:, k - 1, :], a_t[:, k - 1, :], 0.0, ring[:, k - 1, :],
                                                       ALU.is_gt, ALU.min).then_inc(S["p2"], 1)
                dve.wait_ge(S["es"], b + 1)
                for t in range(NT):
                    acc = mm_bank[t // 3][:, (t % 3) * (D + 1):(t % 3 + 1) * (D + 1)]
                    if t == 0:
                        dve.wait_ge(S["mm2"], b + 1)
                    link(nc.vector.tensor_tensor(sm[:, 0, t:t + 1], acc[:, D:D + 1], sm[:, 6, t:t + 1], ALU.add))
                    link(nc.vector.reciprocal(sm[:, 1, t:t + 1], sm[:, 0, t:t + 1]))
                    link(nc.vector.scalar_tensor_tensor(y[:, t, :], acc[:, 0:D], sm[:, 1, t:t + 1], xc[:, t, :],
                                                        ALU.mult, ALU.add))
                    normalise(2, t)
                    if t >= 3:
                        biased(3, t - 3, g)
                apply_norm(2, NT - 1)
                dve.wait_ge(S["dis"], b + 1)
                nc.vector.tensor_tensor(cm[:, :], dis[:, :], mask[:, bass.ts(b, NT)], ALU.mult)
                for t in range(NT - 3, NT):
                    biased(3, t, g)

                dve.wait_ge(S["g3"], b * NT + NT)
                for t in range(NT):
                    bank = mm_bank[t % 2]
                    dve.wait_ge(S["mm3"], b * NT + t + 1)
                    ins = nc.vector.tensor_tensor(y[:, t, :], bank[:, 0:D], g[:, t, 0:D], ALU.add)
                    ins.then_inc(S["mm3_free"], 1)
                    dve.wait_ge(S["mm3_free"], b * NT + t + 1)
                    link(nc.vector.tensor_scalar(y[:, t, :], y[:, t, :], cm[:, t:t + 1], 0.0, ALU.mult, ALU.max))
                    link(nc.vector.tensor_tensor(y[:, t, :], y[:, t, :], xc[:, t, :], ALU.add))
                    normalise(3, t)
                apply_norm(3, NT - 1)
                assert chain[0] == DVE_LINKS, chain[0]

        @block.tensor
        def _(pe):
            mm = nc.tensor.matmul
            pe.wait_ge(S["c_const"], 4)
            pe.wait_ge(S["d_w"], 16 * 7)
            for w in range(7):
                bank, at = w // 4, w % 4
                last = nc.tensor.transpose(psS[:, bank // 2, bank % 2, at * P:(at + 1) * P], w_raw[:, w, :], ident[:, :])
            last.then_inc(S["c_wt_ps"], 1)
            pe.wait_ge(S["d_small"], 16 * 13)
            nc.tensor.transpose(psO[:, 0:6], vrow[:, :], ident[0:6, 0:6]).then_inc(S["c_v_ps"], 1)
            pe.wait_ge(S["c_v"], 1)
            for l in range(2):
                mm(psM[:, 2 * l:2 * l + 2], w_raw[:, 4 + l, :], vcol[:, 2 * l:2 * l + 2], start=True, stop=True)
                last = mm(psM[0:1, 8 + 2 * l:10 + 2 * l], vcol[:, 4 + l:5 + l], vcol[:, 2 * l:2 * l + 2], start=True, stop=True)
            last.then_inc(S["c_u_ps"], 1)
            nc.tensor.transpose(psO[:, 0:B * NT], mask_r[:, :], ident[0:B * NT, 0:B * NT]).then_inc(S["c_mask_ps"], 1)
            pe.wait_ge(S["c_row"], 5)
            rows = brow[:, :, :].rearrange("p l c -> p (l c)")
            mm(psX[:, 0, 0:3 * (D + 2)], ones[:, :], rows[:, 0:3 * (D + 2)], start=True, stop=True)
            mm(psX[:, 1, 0:D + 2], ones[:, :], rows[:, 3 * (D + 2):4 * (D + 2)], start=True, stop=True).then_inc(S["c_bias_ps"], 1)
            pe.wait_ge(S["c_wt"], 2)
            pe.wait_ge(S["c_bias"], 3)

            with pe.Fori(0, B) as b:
                def transpose_tile(layer, t):
                    pe.wait_ge(S["xcur"], b * 4 * NT + (layer - 1) * NT + t + 1)
                    n = (layer - 1) * NT + t
                    if n >= 2:
                        pe.wait_ge(S["xt"], b * 3 * NT + n - 1)
                    nc.tensor.transpose(t_bank[t % 2][:, 0:P], xc[:, t, :], ident[:, :]).then_inc(S["xt_ps"], 1)

                def project(layer, t):
                    pe.wait_ge(S["xt"], b * 3 * NT + (layer - 1) * NT + t + 1)
                    width = D + 2 if layer < 3 else D
                    if t >= 2:
                        if layer == 2:
                            pe.wait_ge(S["g2"], b * NT + t - 1)
                        else:
                            pe.wait_ge(S["hb"], b * 2 * NT + (layer // 3) * NT + t - 1)
                    mm(p_bank[t % 2][:, 0:width], x_t[:, t * P:(t + 1) * P], w_x[:, layer - 1, 0:width],
                       start=True, stop=True).then_inc(S["h_ps"], 1)

                pe.wait_ge(S["d_xin"], b * 16 + 16)
                for t in range(NT):
                    last = nc.tensor.transpose(psS_t[0][:, t, :], x_in[:, t, :], ident[:, :])
                last.then_inc(S["x0_ps"], 1)
                pe.wait_ge(S["x0"], b + 1)
                for w, dst in enumerate((psS[:, 1], psX)):
                    for h in range(2):
                        last = mm(dst[:, h, :], w_t[:, w, :], x_t[:, h * BANK:(h + 1) * BANK], start=True, stop=True)
                    last.then_inc(S["qk_ps"], 1)
                for t in range(NT):
                    last = mm(psS_t[0][:, t, :], x_t[:, t * P:(t + 1) * P], w_t[:, 2, :], start=True, stop=True)
                last.then_inc(S["v_ps"], 1)

                for t in range(NT):
                    pe.wait_ge(d_a[t], b * 16 + 16)
                    if t == 0:
                        pe.wait_ge(S["resid"], b * 2 + 1)
                    elif t == 1:
                        pe.wait_ge(S["v_sb"], b + 1)
                    else:
                        pe.wait_ge(S["at"], b * NT + t - 1)
                    for k in range(NT):
                        last = nc.tensor.transpose(psS_t[(t + 1) % 2][:, k, :], a_nat[:, t, k * P:(k + 1) * P], ident[:, :])
                    last.then_inc(S["at_ps"], 1)

                def max_bank(n):
                    i, m = n // MAXB, n % MAXB
                    gi, qh = i // QH, i % QH
                    j, qt, kh = m // (2 * QT), m // 2 % QT, m % 2
                    h, q0 = HG * gi + j, qh * BANK + qt * P
                    if n >= 2:
                        pe.wait_ge(S["mx"], b * GRP * MAXB + n - 1)
                    mm(psX[:, n % 2, :], qs[0:MROW, h, q0:q0 + P], ks[0:MROW, h, kh * BANK:(kh + 1) * BANK],
                       start=True, stop=True).then_inc(S["mx_ps"], 1)

                def max_rows(i):
                    pe.wait_ge(S["mpart"], b * GRP + i + 1)
                    if i > 1:
                        pe.wait_ge(S["on"], b * GRP + i - 1)
                    for j in range(HG):
                        for qt in range(QT):
                            last = mm(psM[SLOT * j:SLOT * j + 2, qt * P:(qt + 1) * P], mpart[:, j * QT + qt, :],
                                      identb[:, :], start=(qt == 0), stop=(qt == QT - 1), skip_group_check=True,
                                      tile_position=(0, SLOT * j))
                    last.then_inc(S["mrow_ps"], 1)

                def value_products(v):
                    i, kt = v // NT, v % NT
                    if kt == 0 and i > 0:
                        pe.wait_ge(S["ot"], b * GRP + i)
                    if kt in POOL_KT:
                        pe.wait_ge(S["p_pool"], b * GRP * nP + i * nP + (POOL_KT.index(kt) + 1) * (HG // HP))
                    else:
                        pe.wait_ge(S["p_dve"], b * GRP * nD + i * nD + (DVE_KT.index(kt) + 1) * (HG // HP))
                    for j in range(HG):
                        u = v * (HG // HP) + j // HP
                        last = mm(psO[SLOT * j:SLOT * (j + 1), :], vaug[:, kt, HG * (i // QH) + j, :],
                                  ring[:, u % RING, (j % HP) * BANK:(j % HP + 1) * BANK],
                                  start=(kt == 0), stop=(kt == NT - 1), tile_position=(0, SLOT * j), skip_group_check=True)
                    last.then_inc(S["pv"], 1)

                def output_transposes(i):
                    pe.wait_ge(S["ot"], b * GRP + i + 1)
                    if i + 1 < GRP:
                        pe.wait_ge(S["mrow"], b * GRP + i + 1)
                    for t in range(QT):
                        last = nc.tensor.transpose(psM[:, t * P:(t + 1) * P], o_t[:, t * P:(t + 1) * P], ident[:, :])
                    last.then_inc(S["ott_ps"], 1)

                pe.wait_ge(S["d_stack"], b * 16 * 2 * NPROD + 16 * 2 * NPROD)
                pe.wait_ge(S["resid"], b * 2 + 2)
                pe.wait_ge(S["at"], b * NT + NT)
                for n in range(MAXB + AHEAD):
                    max_bank(n)
                max_rows(0)
                for i in range(GRP):
                    gi, qh = i // QH, i % QH
                    pe.wait_ge(S["mrow"], b * GRP + i + 1)
                    for s in range(UN):
                        u = i * UN + s
                        kt, pr = s // (HG // HP), s % (HG // HP)
                        if u >= 2:
                            pe.wait_ge(S["p_exp"], b * GRP * UN + u - 1)
                        for k in range(HP):
                            h = HG * gi + HP * pr + k
                            last = mm(psS[:, u % 2, k, :], ks[:, h, kt * P:(kt + 1) * P],
                                      qs[:, h, qh * BANK:(qh + 1) * BANK], start=True, stop=True)
                        last.then_inc(S["s_ps"], 1)
                        for n in range(MAXB + AHEAD + 2 * u, min(MAXB + AHEAD + 2 * u + 2, GRP * MAXB)):
                            max_bank(n)
                        v = u // (HG // HP) - LAG
                        if pr == 1 and v >= 0:
                            value_products(v)
                        if s == 9 and i > 0:
                            output_transposes(i - 1)
                        if s == UN - AHEAD // 2 + 1 and i + 1 < GRP:
                            max_rows(i + 1)
                for v in range(GRP * NT - LAG, GRP * NT):
                    value_products(v)
                output_transposes(GRP - 1)

                pe.wait_ge(S["on"], b * GRP + GRP)
                for s in range(NT + 4):
                    if s < NT:
                        if s >= 2:
                            pe.wait_ge(S["ont"], b * NT + s - 1)
                        nc.tensor.transpose(psX[:, s % 2, 0:P], y[:, s, :], ident[:, :]).then_inc(S["ont_ps"], 1)
                    if 0 <= s - 1 < NT:
                        t = s - 1
                        pe.wait_ge(S["ont"], b * NT + t + 1)
                        if t >= 2:
                            pe.wait_ge(S["wo_free"], b * NT + t - 1)
                        mm(mm_bank[t % 2][:, 0:D], on_t[:, t * P:(t + 1) * P], w_t[:, 3, :],
                           start=True, stop=True).then_inc(S["wo"], 1)
                    if 0 <= s - 3 < NT:
                        transpose_tile(1, s - 3)
                    if s >= 4:
                        project(1, s - 4)

                def graph_product(t, rhs, width, done, free):
                    if t >= 2:
                        pe.wait_ge(free, b * NT + t - 1)
                    for k in range(NT):
                        last = mm(mm_bank[t % 2][:, 0:width], a_t[:, k, t * P:(t + 1) * P], rhs[:, k, 0:width],
                                  start=(k == 0), stop=(k == NT - 1))
                    last.then_inc(done, 1)

                def aj_row(t):
                    pe.wait_ge(S["ext"], b * 2 * NT + NT + t + 1)
                    return mm(psX_t[:, t, :], ext[:, t, 1:2].to_broadcast([P, P]), ident[:, :], start=True, stop=True)

                pe.wait_ge(S["g1"], b * NT + NT)
                for s in range(NT + 4):
                    if s < NT:
                        graph_product(s, g, D + 2, S["mm1"], S["mm1_free"])
                    if 0 <= s - 2 < NT:
                        transpose_tile(2, s - 2)
                    if 0 <= s - 3 < NT:
                        project(2, s - 3)
                    if s >= 4:
                        last = aj_row(s - 4)
                last.then_inc(S["ajrow_ps"], 1)

                pe.wait_ge(S["w12"], b + 1)
                pe.wait_ge(S["g2"], b * NT + NT)
                for k in range(2):
                    for t in range(NT):
                        last = mm(psS_t[k][:, t, :], w12[:, k, t:t + 1].to_broadcast([P, P]), ident[:, :], start=True, stop=True)
                last.then_inc(S["wrow_ps"], 1)
                for k in range(NT):
                    pe.wait_ge(S["p2"], b * NT + k + 1)
                    for t in range(NT):
                        last = mm(mm_bank[t // 3][:, (t % 3) * (D + 1):(t % 3 + 1) * (D + 1)],
                                  ring[:, k, t * P:(t + 1) * P], g2[:, k, 0:D + 1],
                                  start=(k == 0 and t % 3 == 0), stop=(k == NT - 1), skip_group_check=True)
                last.then_inc(S["mm2"], 1)
                for s in range(NT + 1):
                    if s < NT:
                        transpose_tile(3, s)
                    if s >= 1:
                        project(3, s - 1)

                pe.wait_ge(S["g3"], b * NT + NT)
                for t in range(NT):
                    graph_product(t, g, D, S["mm3"], S["mm3_free"])
                pe.wait_ge(S["mm3_free"], b * NT + NT)


_INS = ['x', 'adj', 'nodemask', 'L0_gnn_Wq', 'L0_gnn_Wk', 'L0_gnn_Wv', 'L0_gnn_Wo', 'L0_gnn_bo',
        'L1_gnn_W_w', 'L1_gnn_W_b', 'L1_gnn_a_w', 'L1_gnn_a_b', 'L2_gnn_W', 'L2_gnn_bW', 'L2_gnn_wai',
        'L2_gnn_bai', 'L2_gnn_waj', 'L2_gnn_baj', 'L3_gnn_W', 'L3_gnn_b']


def kernel(**inputs):
    import numpy as _np
    import concourse.bacc as _bacc
    from concourse import mybir as _mybir
    from concourse.bass_utils import run_bass_kernel_spmd as _run

    nc = _bacc.Bacc("TRN2", target_bir_lowering=False, num_devices=1)
    arrays, args = {}, []
    for name in _INS:
        a = _np.ascontiguousarray(inputs[name])
        arrays[f"in_{name}_dram"] = a
        args.append(nc.dram_tensor(f"in_{name}_dram", a.shape, _mybir.dt.from_np(a.dtype), kind="ExternalInput").ap())
    out = nc.dram_tensor("out_0_dram", inputs['x'].shape, _mybir.dt.from_np(_np.dtype('float32')), kind="ExternalOutput").ap()
    gnn_stack_kernel(nc, *args, out)
    r = _run(nc, [arrays], core_ids=[0])
    return r.results[0]["out_0_dram"]
```

```python
from contextlib import ExitStack

import concourse.bass as bass
from concourse import mybir

F32 = mybir.dt.float32
BF16 = mybir.dt.bfloat16
ACT = mybir.ActivationFunctionType
ALU = mybir.AluOpType

P = 128
BANK = 512
HEADS = 8
HD = 16
HG = 4
HP = 2
SLOT = 32
NPROD = 6
Q_PART = (0, 0, 1, 1, 0, 2)
K_PART = (0, 1, 0, 1, 2, 0)
MROW = NPROD * HD
STK = MROW + 2
RING = 8
POOL_KT = ((0, 3, 6), (0, 3, 6), (0, 3, 6), (0, 3, 6))
AHEAD = 10
LAG = 6
BIG = 9.0e15
SINK = -1.0e9
LN_EPS = 1e-5
ADJ_EPS = 1e-6
DEG_EPS = 1e-8
SLOPE = 0.2
DVE_LINKS = 46


def gnn_stack_kernel(nc, x, adj, nodemask, Wq, Wk, Wv, Wo, bo, W1, b1, a1w, a1b,
                     W2, b2, wai, bai, waj, baj, W3, b3, out):
    B, N, D = x.shape
    NT = N // P
    QH = N // BANK
    GRP = (HEADS // HG) * QH
    QT = BANK // P
    UN = NT * (HG // HP)
    assert D == P and N == 1024 and HEADS * HD == D
    E_KT = POOL_KT[0]
    DVE_KT = tuple(tuple(k for k in range(NT) if k not in g) for g in POOL_KT)
    assert len(POOL_KT) == GRP and all(set(g) <= set(E_KT) for g in POOL_KT)

    def weighed(kts, i, kt):
        return (sum(len(g) for g in kts[:i]) + kts[i].index(kt)) * (HG // HP)

    def pre_maxima(t):
        return range(t * PRE // 2 // NT * 2, (t + 1) * PRE // 2 // NT * 2, 2)

    ALL_P, ALL_D = (sum(len(g) for g in k) * (HG // HP) for k in (POOL_KT, DVE_KT))
    KW = N + BANK
    MAXB = HG * QT * (N // BANK)
    PRE = MAXB + AHEAD
    MX_BANK = [n % 4 if n < PRE else n % 3 for n in range(GRP * MAXB)]
    MX_LAST = [max((m for m in range(n) if MX_BANK[m] == MX_BANK[n]), default=-1) for n in range(GRP * MAXB)]
    PAIRS = GRP * MAXB // 2

    x_v = x.rearrange("b (t p) d -> b p t d", p=P)
    out_v = out.rearrange("b (t p) d -> b p t d", p=P)
    adj_v = adj.rearrange("b (t p) m -> b t p m", p=P)
    qk_dram = [nc.dram_tensor(name, [P, 3, width], BF16, kind="Internal").ap()
               for name, width in (("q_parts", N), ("k_parts", KW))]

    with ExitStack() as ctx:
        def sb(name, shape, dt=F32):
            return ctx.enter_context(nc.sbuf_tensor(name, shape, dt))

        def psum(name, shape):
            return ctx.enter_context(nc.psum_tensor(name, shape, F32))

        def sem(name):
            return ctx.enter_context(nc.semaphore(name))

        ps = psum("ps", [P, 8, BANK])
        s_bank = [ps[:, i] for i in range(3)]
        x_bank = [ps[:, 3 + i] for i in range(3)]
        pre_bank = x_bank + [s_bank[2]]
        o_bank, m_bank = ps[:, 6], ps[:, 7]

        def double(i):
            return ps[:, i:i + 2].rearrange("p a c -> p (a c)"), ps[:, i:i + 2].rearrange("p a (t c) -> p (a t) c", c=P)

        (d0, d0_t), (d2, d2_t), (d4, d4_t), (d6, d6_t) = double(0), double(2), double(4), double(6)
        at_t = (d6_t, d0_t)
        mm_bank = [ps[:, 6], ps[:, 7], ps[:, 4]]
        t_bank = [ps[:, 0], ps[:, 1]]
        p_bank = [ps[:, 2], ps[:, 3]]

        a_nat = sb("a_nat", [P, NT, N])
        a_t = sb("a_t", [P, NT, N])
        a_te = sb("a_te", [P, len(E_KT), N])
        pen = sb("pen", [P, NT, N], BF16)
        qs = sb("qs", [STK, HEADS, N], BF16)
        ks = sb("ks", [STK, HEADS, KW], BF16)
        ring = sb("ring", [P, RING, 2 * BANK])
        x_in = sb("x_in", [P, NT, D])
        xc = sb("xc", [P, NT, D])
        y = sb("y", [P, NT, D])
        x_t = sb("x_t", [P, N])
        vaug = sb("vaug", [P, NT, HEADS, SLOT])
        g = sb("g", [P, NT, D + 2])
        g2 = sb("g2", [P, NT, D + 2])
        o_t = sb("o_t", [P, BANK])
        ident = sb("ident", [P, P])
        identb = sb("identb", [P, P], BF16)
        w_t = sb("w_t", [P, 5, D])
        w_x = sb("w_x", [P, 3, D + 2])
        vcol = sb("vcol", [P, 6])
        bias = sb("bias", [P, 4, D + 2])
        mask = sb("mask", [P, B * NT])
        ones = sb("ones", [1, P])
        mrow = sb("mrow", [P, 2, HG * QT])
        carrier = sb("carrier", [P, 8])
        mpart = sb("mpart", [P, HG * QT, 2], BF16)
        rden = sb("rden", [P, QT, HG])
        st = sb("st", [P, NT, 6])
        mv = sb("mv", [P, NT, 2])
        var = sb("var", [P, NT])
        rstd = sb("rstd", [P, NT])
        mhalf = sb("mhalf", [P, NT])
        ext = sb("ext", [P, NT, 2])
        eexp = sb("eexp", [P, NT, 2])
        deg = sb("deg", [P, NT])
        dis = sb("dis", [P, NT])
        cm = sb("cm", [P, NT])
        sm = sb("sm", [P, 8, NT])
        w12 = sb("w12", [P, 2, NT])
        y_f = y[:, :, :].rearrange("p t d -> p (t d)")
        brow = y_f[0:1, 0:4 * (D + 2)].rearrange("p (l c) -> p l c", l=4)
        vrow = y_f[0:6, 5 * D:6 * D]
        mask_r = y_f[0:B * NT, 6 * D:7 * D]
        w_raw = ring[:, 0:1, 0:7 * D].rearrange("p a (w d) -> p (a w) d", d=D)
        on_t = [g2[:, t, 0:D] for t in range(NT)]
        over = [x_t[:, i * BANK:(i + 1) * BANK] for i in range(2)]
        work = a_nat[:, :, :].rearrange("p t n -> p (t n)")
        cuts = [0]
        for width in (N, N, KW, 3 * N // 2, 3 * KW // 2):
            cuts.append(cuts[-1] + width)
        assert cuts[-1] <= NT * N
        x_t0, q32, k32, q_parts, k_parts = (work[:, a:z] for a, z in zip(cuts, cuts[1:]))
        res = [q32, k32]
        qkp = [part.bitcast(BF16).rearrange("p (k n) -> p k n", k=3) for part in (q_parts, k_parts)]

        S = {n: sem(n) for n in (
            "d_w d_small d_xin d_parts d_stack d_out c_const c_wt_ps c_wt c_v_ps c_v c_u_ps c_u c_mask_ps c_row c_bias_ps c_bias "
            "xt_ps xt x0_ps x0 xb qk_ps v_ps qk z1 resid z2q z2k z3 v_sb at_ps at pen ate mx_ps over mx mpart mrow_ps mrow "
            "s_ps p_exp p_dve p_pool pv ot ott_ps on ont_ps ont wo xcur var rstd h_ps hb ext expf g1 g2 g3 mm1 "
            "ajrow_ps w12 wrow_ps t2 t e2 p2 mm2 es deg dis mm3 mm3_free y stats aggr "
            "dve pool").split()}
        d_a = [sem(f"d_a{t}") for t in range(NT)]

        block = ctx.enter_context(nc.Block())

        @block.sync
        def _(sp):
            sp.dma_start(x_in[:, :, :], x_v[0]).then_inc(S["d_xin"], 16)
            for w, src in enumerate((Wq, Wk, Wv, Wo, W1, W2, W3)):
                sp.dma_start(w_raw[:, w, :], src).then_inc(S["d_w"], 16)
            sp.dma_start(vrow[0:2, :], a1w.rearrange("(k e) -> k e", k=2)).then_inc(S["d_small"], 16)
            sp.dma_start(vrow[2:3, :], wai).then_inc(S["d_small"], 16)
            sp.dma_start(vrow[3:4, :], waj).then_inc(S["d_small"], 16)
            for i, v in enumerate((b1, b2)):
                sp.dma_start(vrow[4 + i:5 + i, :], v.rearrange("(k e) -> k e", k=1)).then_inc(S["d_small"], 16)
            for i, v in enumerate((bo, b1, b2, b3)):
                sp.dma_start(brow[:, i, 0:D], v.rearrange("(k e) -> k e", k=1)).then_inc(S["d_small"], 16)
            for i, (row, col, v) in enumerate(((1, D, a1b), (2, D, bai), (2, D + 1, baj))):
                sp.dma_start(brow[:, row, col:col + 1], v.rearrange("(k e) -> k e", k=1)).then_inc(S["d_small"], 16)
            sp.dma_start(mask_r[:, :], nodemask.rearrange("b (t p) -> (b t) p", p=P)).then_inc(S["d_small"], 16)
            def load_adj(n):
                for t in range(NT):
                    sp.dma_start(a_nat[:, t, :], adj_v[n, t]).then_inc(d_a[t], 16)

            def stack_parts(b):
                for i in range(2):
                    sp.wait_ge(S["z3"], b * 2 + i + 1)
                    sp.dma_start(qk_dram[i], qkp[i]).then_inc(S["d_parts"], 16)
                sp.wait_ge(S["d_parts"], b * 32 + 16 * 2)
                for i, (stack, part) in enumerate(((qs, Q_PART), (ks, K_PART))):
                    for j in range(NPROD):
                        src = qk_dram[i][:, part[j], :].rearrange("(h r) n -> r h n", r=HD)
                        sp.dma_start(stack[HD * j:HD * (j + 1), :, :], src).then_inc(S["d_stack"], 16)

            def store_graph(b):
                sp.wait_ge(S["xcur"], b * 4 * NT + 4 * NT)
                sp.dma_start(out_v[b], xc[:, :, :]).then_inc(S["d_out"], 16)

            stack_parts(0)
            sp.wait_ge(S["v_sb"], 1)
            load_adj(0)
            with sp.Fori(0, B - 1) as b:
                sp.wait_ge(S["xcur"], b * 4 * NT + NT)
                sp.dma_start(x_in[:, :, :], x_v[b + 1]).then_inc(S["d_xin"], 16)
                stack_parts(b + 1)
                sp.wait_ge(S["v_sb"], b + 2)
                load_adj(b + 1)
                store_graph(b)
            store_graph(B - 1)
            sp.wait_ge(S["d_out"], B * 16 + 16)

        @block.gpsimd
        def _(pool):
            nc.gpsimd.memset(ident[:, :], 0.0).then_inc(S["pool"], 1)
            nc.gpsimd.memset(mhalf[:, :], -0.5).then_inc(S["pool"], 1)
            nc.gpsimd.memset(vaug[:, :, :, :], 0.0).then_inc(S["pool"], 1)
            pool.wait_ge(S["pool"], 3)
            nc.gpsimd.affine_select(out=ident[:, :], in_=ident[:, :], compare_op=ALU.not_equal, fill=1.0,
                                    base=0, pattern=[[-1, P]], channel_multiplier=1).then_inc(S["pool"], 1)
            nc.gpsimd.memset(vaug[:, :, :, HD:HD + 1], 1.0).then_inc(S["c_const"], 1)
            pool.wait_ge(S["pool"], 4)
            nc.gpsimd.tensor_copy(identb[:, :], ident[:, :]).then_inc(S["c_const"], 1)

            def split(n):
                for i in range(2):
                    pool.wait_ge(S["z1"], n * 2 + i + 1)
                    nc.gpsimd.tensor_tensor(res[i], res[i], qkp[i][:, 0, :], ALU.subtract).then_inc(S["resid"], 1)
                for i in range(2):
                    pool.wait_ge(S["z2k" if i else "z2q"], n + 1)
                    nc.gpsimd.tensor_tensor(qkp[i][:, 2, :], res[i], qkp[i][:, 1, :], ALU.subtract).then_inc(S["z3"], 1)

            def graph(b, more):
                def inv_sqrt(layer):
                    for t in range(NT):
                        pool.wait_ge(S["var"], b * 4 * NT + layer * NT + t + 1)
                        nc.gpsimd.tensor_tensor(rstd[:, t:t + 1], var[:, t:t + 1], mhalf[:, t:t + 1],
                                                ALU.pow).then_inc(S["rstd"], 1)

                pool.wait_ge(S["at"], b * NT + NT)
                pool.wait_ge(S["x0_ps"], b + 1)
                nc.gpsimd.tensor_tensor(x_in[:, :, :], x_in[:, :, :], bias[:, 0:1, 0:D].to_broadcast([P, NT, D]),
                                        ALU.add).then_inc(S["xb"], 1)
                for n, kt in enumerate(E_KT):
                    nc.gpsimd.tensor_scalar(a_te[:, n, :], a_t[:, kt, :], 1.0, ADJ_EPS, ALU.mult, ALU.add).then_inc(S["ate"], 1)
                pool.wait_ge(S["ate"], (b + 1) * len(E_KT))
                for i in range(GRP):
                    qh = i % QH
                    for kt in POOL_KT[i]:
                        n = E_KT.index(kt)
                        for pr in range(HG // HP):
                            u = i * UN + kt * (HG // HP) + pr
                            tile = ring[:, u % RING, :].rearrange("p (h q) -> p h q", h=HP)
                            e = a_te[:, n, qh * BANK:(qh + 1) * BANK].unsqueeze(1).to_broadcast([P, HP, BANK])
                            pool.wait_ge(S["p_exp"], (b * GRP * UN + u + 1) * HP)
                            nc.gpsimd.tensor_tensor(tile, tile, e, ALU.mult).then_inc(S["p_pool"], 1)
                inv_sqrt(0)
                inv_sqrt(1)
                pool.wait_ge(S["deg"], b + 1)
                nc.gpsimd.tensor_tensor(dis[:, :], deg[:, :], mhalf[:, :], ALU.pow).then_inc(S["dis"], 1)
                if more:
                    split(b + 1)
                inv_sqrt(2)
                inv_sqrt(3)

            split(0)
            pool.wait_ge(S["c_bias"], 3)
            with pool.Fori(0, B - 1) as b:
                graph(b, True)
            graph(B - 1, False)

        @block.scalar
        def _(act):
            act.wait_ge(S["c_wt_ps"], 1)
            nc.scalar.copy(w_t[:, 0:4, :], ps[:, 0].rearrange("p (t c) -> p t c", c=D)).then_inc(S["c_wt"], 1)
            nc.scalar.activation(w_t[:, 4, :], ps[:, 0, D:2 * D], ACT.Copy, scale=-1.0).then_inc(S["c_wt"], 1)
            nc.scalar.copy(w_x[:, :, 0:D], ps[:, 1].rearrange("p (t c) -> p t c", c=D)[:, 0:3, :]).then_inc(S["c_wt"], 1)
            def prepare(n):
                act.wait_ge(S["x0_ps"], n + 1)
                nc.scalar.copy(x_t0, d0).then_inc(S["x0"], 1)
                act.wait_ge(S["qk_ps"], n * 3 + 1)
                nc.scalar.activation(q32, d2, ACT.Copy, scale=1.0 / HD ** 0.5).then_inc(S["qk"], 1)
                act.wait_ge(S["qk"], n * 3 + 1)
                nc.scalar.copy(qkp[0][:, 0, :], q32).then_inc(S["z1"], 1)
                act.wait_ge(S["qk_ps"], n * 3 + 2)
                nc.scalar.copy(k32[:, 0:N], d6).then_inc(S["qk"], 1)
                act.wait_ge(S["qk_ps"], n * 3 + 3)
                nc.scalar.copy(k32[:, N:KW], ps[:, 2]).then_inc(S["qk"], 1)
                act.wait_ge(S["qk"], n * 3 + 3)
                nc.scalar.copy(qkp[1][:, 0, :], k32).then_inc(S["z1"], 1)
                act.wait_ge(S["v_ps"], n + 1)
                nc.scalar.copy(vaug[:, :, :, 0:HD],
                               d0_t.rearrange("p t (h d) -> p t h d", d=HD)).then_inc(S["v_sb"], 1)
                act.wait_ge(S["resid"], n * 2 + 1)
                nc.scalar.copy(qkp[0][:, 1, :], res[0]).then_inc(S["z2q"], 1)

            prepare(0)
            act.wait_ge(S["c_v_ps"], 1)
            nc.scalar.copy(vcol[:, :], o_bank[:, 0:6]).then_inc(S["c_v"], 1)
            act.wait_ge(S["c_u_ps"], 1)
            nc.scalar.copy(w_x[:, 0:2, D:D + 2], m_bank[:, 0:4].rearrange("p (l k) -> p l k", l=2)).then_inc(S["c_u"], 1)
            act.wait_ge(S["c_bias_ps"], 1)
            nc.scalar.copy(bias[:, 0:3, :], ps[:, 4, 0:3 * (D + 2)].rearrange("p (l c) -> p l c", l=3)).then_inc(S["c_bias"], 1)
            nc.scalar.copy(bias[:, 3, :], ps[:, 5, 0:D + 2]).then_inc(S["c_bias"], 1)
            act.wait_ge(S["c_mask_ps"], 1)
            nc.scalar.copy(mask[:, :], o_bank[:, 0:B * NT]).then_inc(S["c_bias"], 1)

            def graph(b, more):
                def xt_copy(layer, t):
                    act.wait_ge(S["xt_ps"], b * 3 * NT + (layer - 1) * NT + t + 1)
                    nc.scalar.copy(x_t[:, t * P:(t + 1) * P], t_bank[t % 2][:, 0:P]).then_inc(S["xt"], 1)

                def rows_copy(half):
                    act.wait_ge(S["ont_ps"], b * 2 + half + 1)
                    nc.scalar.copy(g2[:, half * QT:(half + 1) * QT, 0:D],
                                   ps[:, (3, 6)[half]].rearrange("p (t c) -> p t c", c=P)).then_inc(S["ont"], 1)

                def exp_rows(t):
                    act.wait_ge(S["ext"], b * 2 * NT + t + 2)
                    nc.scalar.activation(eexp[:, t:t + 2, :], ext[:, t:t + 2, :], ACT.Exp).then_inc(S["expf"], 2)
                    act.wait_ge(S["expf"], b * NT + t + 2)
                    nc.scalar.copy(g[:, t:t + 2, D:D + 1], eexp[:, t:t + 2, 1:2])
                    for k in (t, t + 1):
                        act.wait_ge(S["hb"], b * 2 * NT + k + 1)
                        nc.scalar.activation(g[:, k, 0:D], g[:, k, 0:D], ACT.Copy, scale=eexp[:, k, 1:2]).then_inc(S["g1"], 1)

                def scale_rows(t):
                    act.wait_ge(S["hb"], b * 2 * NT + NT + t + 1)
                    nc.scalar.activation(g[:, t, 0:D], g[:, t, 0:D], ACT.Copy, scale=dis[:, t:t + 1]).then_inc(S["g3"], 1)

                def positive_part(n):
                    act.wait_ge(S["mx_ps"], b * GRP * MAXB + n + 1)
                    if n >= 4:
                        act.wait_ge(S["mx"], b * PAIRS + n // 2 - 1)
                    nc.scalar.activation(over[n // 2 % 2], pre_bank[MX_BANK[n]], ACT.Relu).then_inc(S["over"], 1)

                def max_rows(i):
                    gi, qh = i // QH, i % QH
                    act.wait_ge(S["mrow_ps"], b * GRP + i + 1)
                    for j in range(HG):
                        last = nc.scalar.copy(qs[MROW:STK, HG * gi + j, qh * BANK:(qh + 1) * BANK],
                                              m_bank[SLOT * j:SLOT * j + 2, :])
                    last.then_inc(S["mrow"], 1)

                for t in range(NT):
                    if t > 0:
                        positive_part(pre_maxima(t)[0])
                    act.wait_ge(S["at_ps"], b * NT + t + 1)
                    nc.scalar.copy(a_t[:, :, t * P:(t + 1) * P], at_t[t % 2]).then_inc(S["at"], 1)
                    if t == NT - 1:
                        max_rows(0)
                    for n in pre_maxima(t)[min(t, 1):]:
                        positive_part(n)
                for i in range(GRP):
                    for s in range(UN):
                        u = i * UN + s
                        if u >= RING:
                            act.wait_ge(S["pv"], b * GRP * UN + u - RING + 1)
                        for n in range(HP * u, HP * (u + 1)):
                            act.wait_ge(S["s_ps"], b * GRP * UN * HP + n + 1)
                            nc.scalar.activation(ring[:, u % RING, (n % HP) * BANK:(n % HP + 1) * BANK],
                                                 s_bank[n % 3], ACT.Exp).then_inc(S["p_exp"], 1)
                        if PRE // 2 + u < PAIRS:
                            positive_part(PRE + 2 * u)
                        if s == LAG - 1 and i > 0:
                            act.wait_ge(S["pv"], b * GRP * UN + i * UN)
                            nc.scalar.copy(o_t[:, :], o_bank[:, :]).then_inc(S["ot"], 1)
                        if s == UN - AHEAD // 2 + 3 and i + 1 < GRP:
                            max_rows(i + 1)
                        if s == 13 and i + 1 == GRP:
                            rows_copy(0)
                act.wait_ge(S["pv"], b * GRP * UN + GRP * UN)
                nc.scalar.copy(o_t[:, :], o_bank[:, :]).then_inc(S["ot"], 1)

                xt_copy(1, 0)
                xt_copy(1, 1)
                rows_copy(1)
                for s in range(2, NT + 3):
                    if s < NT:
                        xt_copy(1, s)
                    if s >= 4 and s % 2 == 0:
                        exp_rows(s - 4)
                for t in range(NT):
                    xt_copy(2, t)
                if more:
                    prepare(b + 1)
                act.wait_ge(S["w12"], b + 1)
                nc.scalar.activation(sm[:, 6, :], sm[:, 5, :], ACT.Exp).then_inc(S["es"], 1)
                act.wait_ge(S["wrow_ps"], b * 2 + 1)
                for k in range(NT + 1):
                    if k < NT:
                        nc.scalar.activation(ring[:, k, :], d2, ACT.Identity,
                                             bias=sm[:, 7, k:k + 1]).then_inc(S["t2"], 1)
                    if k > 0:
                        act.wait_ge(S["t"], b * NT + k)
                        nc.scalar.activation(ring[:, k - 1, :], ring[:, k - 1, :], ACT.Exp).then_inc(S["e2"], 1)
                act.wait_ge(S["dis"], b + 1)
                for s in range(NT + 3):
                    if s < NT:
                        xt_copy(3, s)
                    if s >= 3:
                        scale_rows(s - 3)

            with act.Fori(0, B - 1) as b:
                graph(b, True)
            graph(B - 1, False)

        @block.vector
        def _(dve):
            nc.vector.memset(ones[:, :], 1.0).then_inc(S["c_const"], 1)
            nc.vector.memset(xc[:, :, :], 0.0).then_inc(S["d_out"], 16)
            nc.vector.memset(ks[MROW:STK, :, :], 1.0).then_inc(S["c_const"], 1)
            def second_part(n):
                dve.wait_ge(S["resid"], n * 2 + 2)
                nc.vector.tensor_copy(qkp[1][:, 1, :], res[1]).then_inc(S["z2k"], 1)

            second_part(0)
            dve.wait_ge(S["c_u"], 1)
            dve.wait_ge(S["d_small"], 16 * 13)
            nc.vector.tensor_tensor(brow[:, 1, D:D + 1], brow[:, 1, D:D + 1], m_bank[0:1, 8:9], ALU.add).then_inc(S["c_row"], 1)
            nc.vector.tensor_copy(brow[:, 1, D + 1:D + 2], m_bank[0:1, 9:10]).then_inc(S["c_row"], 1)
            nc.vector.tensor_tensor(brow[:, 2, D:D + 2], brow[:, 2, D:D + 2], m_bank[0:1, 10:12], ALU.add).then_inc(S["c_row"], 1)
            nc.vector.memset(brow[:, 0, D:D + 2], 0.0).then_inc(S["c_row"], 1)
            nc.vector.memset(brow[:, 3, D:D + 2], 0.0).then_inc(S["c_row"], 1)
            nc.vector.memset(g[:, :, D + 1], 1.0).then_inc(S["dve"], 1)
            nc.vector.memset(g2[:, :, D], 1.0).then_inc(S["dve"], 1)
            dve.wait_ge(S["dve"], 2)

            def graph(b, more):
                chain = [0]

                def link(ins):
                    chain[0] += 1
                    ins.then_inc(S["dve"], 1)
                    dve.wait_ge(S["dve"], b * DVE_LINKS + chain[0] + 2)

                def apply_norm(layer, t):
                    if layer == 0 and t == 0:
                        dve.wait_ge(S["d_out"], b * 16 + 16)
                    dve.wait_ge(S["rstd"], b * 4 * NT + layer * NT + t + 1)
                    nc.vector.tensor_scalar(xc[:, t, :], y[:, t, :], mv[:, t, 0:1], rstd[:, t:t + 1],
                                            ALU.subtract, ALU.mult).then_inc(S["xcur"], 1)

                def normalise(layer, make_y, project=None, first=0, end=NT + 4):
                    base = b * 4 * NT + layer * NT
                    for s in range(first, end):
                        if 1 <= s <= NT:
                            dve.wait_ge(S["stats"], base + s)
                        if s < NT:
                            make_y(s).then_inc(S["y"], 1)
                        elif s == NT:
                            nc.vector.memset(carrier[:, 4 + layer:5 + layer], 0.0)
                        if 1 <= s <= NT:
                            nc.vector.bn_aggr(mv[:, s - 1, :], st[:, s - 1, :]).then_inc(S["aggr"], 1)
                        if s < NT:
                            dve.wait_ge(S["y"], base + s + 1)
                            nc.vector.bn_stats(st[:, s, :], y[:, s, :]).then_inc(S["stats"], 1)
                        if 1 <= s <= NT:
                            dve.wait_ge(S["aggr"], base + s)
                            nc.vector.tensor_scalar(var[:, s - 1:s], mv[:, s - 1, 1:2], LN_EPS, None, ALU.add).then_inc(S["var"], 1)
                        if 2 <= s <= NT + 1:
                            apply_norm(layer, s - 2)
                        if project and s >= 4:
                            project(s - 4)

                def biased(layer, t, dst):
                    bank = p_bank[t % 2]
                    dve.wait_ge(S["h_ps"], b * 3 * NT + (layer - 1) * NT + t + 1)
                    if layer < 3:
                        nc.vector.tensor_tensor(ext[:, t, :], bank[:, D:D + 2], bias[:, layer, D:D + 2],
                                                ALU.add).then_inc(S["ext"], 1)
                    nc.vector.tensor_tensor(dst[:, t, 0:D], bank[:, 0:D], bias[:, layer, 0:D],
                                            ALU.add).then_inc(S["g2" if layer == 2 else "hb"], 1)

                def max_pair(n):
                    m = n % MAXB
                    diff = over[n // 2 % 2]
                    dve.wait_ge(S["over"], b * PAIRS + n // 2 + 1)
                    dve.wait_ge(S["mx_ps"], b * GRP * MAXB + n + 2)
                    nc.vector.memset(carrier[:, n // 2 % 4:n // 2 % 4 + 1], 0.0)
                    nc.vector.tensor_tensor_reduce(out=diff, in0=diff, in1=pre_bank[MX_BANK[n + 1]], scale=1.0, scalar=-3.0e38,
                                                   op0=ALU.add, op1=ALU.max,
                                                   accum_out=mrow[:, n // MAXB % 2, m // 2:m // 2 + 1]).then_inc(S["mx"], 1)

                def max_parts(i):
                    dve.wait_ge(S["mx"], b * PAIRS + (i + 1) * MAXB // 2)
                    link(nc.vector.tensor_scalar(mpart[:, :, 0], mrow[:, i % 2, :], -1.0, None, ALU.mult))
                    nc.vector.scalar_tensor_tensor(mpart[:, :, 1], mrow[:, i % 2, :], -1.0, mpart[:, :, 0],
                                                   ALU.mult, ALU.subtract).then_inc(S["mpart"], 1)

                def attention_out(i):
                    gi, qh = i // QH, i % QH
                    dve.wait_ge(S["ott_ps"], b * GRP + i + 1)
                    v = m_bank[:, :].rearrange("p (t j c) -> p t j c", t=QT, j=HG)
                    link(nc.vector.reciprocal(rden[:, :, :], v[:, :, :, HD]))
                    o = y[:, qh * QT:(qh + 1) * QT, gi * HG * HD:(gi + 1) * HG * HD].rearrange("p t (j d) -> p t j d", d=HD)
                    nc.vector.tensor_tensor(o, v[:, :, :, 0:HD], rden[:, :, :].unsqueeze(3).to_broadcast([P, QT, HG, HD]),
                                            ALU.mult).then_inc(S["on"], 1)

                def weigh(u):
                    i, kt = u // UN, u % UN // (HG // HP)
                    if kt in DVE_KT[i]:
                        qh = i % QH
                        tile = ring[:, u % RING, :].rearrange("p (h q) -> p h q", h=HP)
                        e = a_t[:, kt, qh * BANK:(qh + 1) * BANK].unsqueeze(1).to_broadcast([P, HP, BANK])
                        dve.wait_ge(S["p_exp"], (b * GRP * UN + u + 1) * HP)
                        nc.vector.scalar_tensor_tensor(tile, e, ADJ_EPS, tile, ALU.add, ALU.mult).then_inc(S["p_dve"], 1)

                for t in range(NT):
                    for n in pre_maxima(t):
                        max_pair(n)
                        if (n + 2) % MAXB == 0:
                            max_parts(n // MAXB)
                dve.wait_ge(S["at"], b * NT + NT)
                for u in range(GRP * UN):
                    n = PRE + 2 * u
                    if n < GRP * MAXB:
                        max_pair(n)
                        if (n + 2) % MAXB == 0:
                            max_parts(n // MAXB)
                    if u >= 2:
                        weigh(u - 2)
                    if 0 <= u - PAIRS + PRE // 2 - 1 < NT:
                        t = u - PAIRS + PRE // 2 - 1
                        dve.wait_ge(d_a[t], b * 16 + 16)
                        nc.vector.tensor_scalar(pen[:, t, :], a_nat[:, t, :], 0.0, -BIG, ALU.is_le, ALU.mult).then_inc(S["pen"], 1)
                    if u % UN == 9 and u > UN:
                        attention_out(u // UN - 1)
                weigh(GRP * UN - 2)
                weigh(GRP * UN - 1)

                def attended(t):
                    dve.wait_ge(S["wo"], b * 2 + t // QT + 1)
                    return nc.vector.tensor_tensor(y[:, t, :], d4_t[:, t, :], x_in[:, t, :], ALU.add)

                dve.wait_ge(S["xb"], b + 1)
                normalise(0, attended, end=QT)
                attention_out(GRP - 1)
                normalise(0, attended, lambda t: biased(1, t, g), first=QT)

                dve.wait_ge(S["expf"], b * NT + NT)
                def averaged(t):
                    bank = mm_bank[t % 2]
                    dve.wait_ge(S["mm1"], b * NT + t + 1)
                    link(nc.vector.tensor_tensor(sm[:, 0, t:t + 1], bank[:, D:D + 1], eexp[:, t, 0:1], ALU.mult))
                    link(nc.vector.reciprocal(sm[:, 1, t:t + 1], sm[:, 0, t:t + 1]))
                    link(nc.vector.tensor_tensor(sm[:, 2, t:t + 1], sm[:, 1, t:t + 1], eexp[:, t, 0:1], ALU.mult))
                    ins = nc.vector.tensor_scalar(deg[:, t:t + 1], bank[:, D + 1:D + 2], 1.0, DEG_EPS, ALU.add, ALU.add)
                    if t == NT - 1:
                        ins.then_inc(S["deg"], 1)
                    return nc.vector.scalar_tensor_tensor(y[:, t, :], bank[:, 0:D], sm[:, 2, t:t + 1], xc[:, t, :], ALU.mult, ALU.add)

                normalise(1, averaged, lambda t: biased(2, t, g2))

                dve.wait_ge(S["ext"], b * 2 * NT + 2 * NT)
                nc.vector.tensor_scalar(sm[:, 7, :], ext[:, :, 1], SLOPE, None, ALU.mult)
                dve.wait_ge(S["ajrow_ps"], b + 1)
                nc.vector.memset(carrier[:, 3:4], 0.0)
                for t in range(NT):
                    ins = nc.vector.tensor_tensor_reduce(out=ring[:, t, :], in0=pen[:, t, :], in1=d4, scale=1.0,
                                                         scalar=-3.0e38, op0=ALU.add, op1=ALU.max,
                                                         accum_out=sm[:, 0, t:t + 1])
                link(ins)
                link(nc.vector.tensor_tensor(sm[:, 1, :], sm[:, 0, :], ext[:, :, 0], ALU.add))
                link(nc.vector.scalar_tensor_tensor(sm[:, 2, :], sm[:, 1, :], SLOPE, sm[:, 1, :], ALU.mult, ALU.max))
                link(nc.vector.tensor_scalar(sm[:, 3, :], sm[:, 2, :], SINK, None, ALU.max))
                nc.vector.tensor_tensor(w12[:, 0, :], ext[:, :, 0], sm[:, 3, :], ALU.subtract)
                nc.vector.scalar_tensor_tensor(w12[:, 1, :], ext[:, :, 0], SLOPE, sm[:, 3, :], ALU.mult, ALU.subtract)
                nc.vector.tensor_scalar(sm[:, 5, :], sm[:, 3, :], -1.0, SINK, ALU.mult, ALU.add).then_inc(S["w12"], 1)
                if more:
                    second_part(b + 1)
                dve.wait_ge(S["wrow_ps"], b * 2 + 2)
                for k in range(NT + 1):
                    if k < NT:
                        dve.wait_ge(S["t2"], b * NT + k + 1)
                        nc.vector.scalar_tensor_tensor(ring[:, k, :], d0, ext[:, k, 1:2], ring[:, k, :],
                                                       ALU.add, ALU.max).then_inc(S["t"], 1)
                    if k > 0:
                        dve.wait_ge(S["e2"], b * NT + k)
                        nc.vector.scalar_tensor_tensor(ring[:, k - 1, :], a_t[:, k - 1, :], 0.0, ring[:, k - 1, :],
                                                       ALU.is_gt, ALU.min).then_inc(S["p2"], 1)
                dve.wait_ge(S["es"], b + 1)
                dve.wait_ge(S["mm2"], b + 1)
                for i, t in enumerate(range(0, NT, 3)):
                    n = min(3, NT - t)
                    den = mm_bank[i][:, 0:n * (D + 1)].rearrange("p (t c) -> p t c", c=D + 1)[:, :, D]
                    ins = nc.vector.tensor_tensor(sm[:, 0, t:t + n], den, sm[:, 6, t:t + n], ALU.add)
                link(ins)
                link(nc.vector.reciprocal(sm[:, 1, :], sm[:, 0, :]))

                def attended2(t):
                    acc = mm_bank[t // 3][:, (t % 3) * (D + 1):(t % 3 + 1) * (D + 1)]
                    return nc.vector.scalar_tensor_tensor(y[:, t, :], acc[:, 0:D], sm[:, 1, t:t + 1], xc[:, t, :], ALU.mult, ALU.add)

                normalise(2, attended2, lambda t: biased(3, t, g))
                dve.wait_ge(S["dis"], b + 1)
                nc.vector.tensor_tensor(cm[:, :], dis[:, :], mask[:, bass.ts(b, NT)], ALU.mult)

                dve.wait_ge(S["g3"], b * NT + NT)
                def convolved(t):
                    dve.wait_ge(S["mm3"], b * NT + t + 1)
                    ins = nc.vector.tensor_tensor(y[:, t, :], mm_bank[t % 2][:, 0:D], g[:, t, 0:D], ALU.add)
                    ins.then_inc(S["mm3_free"], 1)
                    dve.wait_ge(S["mm3_free"], b * NT + t + 1)
                    link(nc.vector.tensor_scalar(y[:, t, :], y[:, t, :], cm[:, t:t + 1], 0.0, ALU.mult, ALU.max))
                    return nc.vector.tensor_tensor(y[:, t, :], y[:, t, :], xc[:, t, :], ALU.add)

                normalise(3, convolved)
                assert chain[0] == DVE_LINKS, chain[0]

            with dve.Fori(0, B - 1) as b:
                graph(b, True)
            graph(B - 1, False)

        @block.tensor
        def _(pe):
            mm = nc.tensor.matmul
            pe.wait_ge(S["c_const"], 4)
            pe.wait_ge(S["d_w"], 16 * 7)
            for w in range(7):
                bank, at = w // 4, w % 4
                last = nc.tensor.transpose(ps[:, bank, at * P:(at + 1) * P], w_raw[:, w, :], ident[:, :])
            last.then_inc(S["c_wt_ps"], 1)
            def prepare(n):
                pe.wait_ge(S["d_xin"], n * 16 + 16)
                for t in range(NT):
                    last = nc.tensor.transpose(d0_t[:, t, :], x_in[:, t, :], ident[:, :])
                last.then_inc(S["x0_ps"], 1)
                pe.wait_ge(S["x0"], n + 1)
                for w, dst in enumerate((2, 6)):
                    for h in range(2):
                        last = mm(ps[:, dst + h], w_t[:, w, :], x_t0[:, h * BANK:(h + 1) * BANK], start=True, stop=True)
                    last.then_inc(S["qk_ps"], 1)
                pe.wait_ge(S["qk"], n * 3 + 1)
                for h, w in ((0, 1), (1, 4)):
                    last = mm(ps[:, 2], w_t[:, w, :], x_t0[:, h * BANK:(h + 1) * BANK], start=(h == 0), stop=(h == 1))
                last.then_inc(S["qk_ps"], 1)
                for t in range(NT):
                    last = mm(d0_t[:, t, :], x_t0[:, t * P:(t + 1) * P], w_t[:, 2, :], start=True, stop=True)
                last.then_inc(S["v_ps"], 1)

            pe.wait_ge(S["c_wt"], 3)
            prepare(0)
            pe.wait_ge(S["v_sb"], 1)
            pe.wait_ge(S["d_small"], 16 * 13)
            nc.tensor.transpose(o_bank[:, 0:6], vrow[:, :], ident[0:6, 0:6]).then_inc(S["c_v_ps"], 1)
            pe.wait_ge(S["c_v"], 1)
            for l in range(2):
                mm(m_bank[:, 2 * l:2 * l + 2], w_raw[:, 4 + l, :], vcol[:, 2 * l:2 * l + 2], start=True, stop=True)
                last = mm(m_bank[0:1, 8 + 2 * l:10 + 2 * l], vcol[:, 4 + l:5 + l], vcol[:, 2 * l:2 * l + 2], start=True, stop=True)
            last.then_inc(S["c_u_ps"], 1)
            nc.tensor.transpose(o_bank[:, 0:B * NT], mask_r[:, :], ident[0:B * NT, 0:B * NT]).then_inc(S["c_mask_ps"], 1)
            pe.wait_ge(S["c_row"], 5)
            rows = brow[:, :, :].rearrange("p l c -> p (l c)")
            mm(ps[:, 4, 0:3 * (D + 2)], ones[:, :], rows[:, 0:3 * (D + 2)], start=True, stop=True)
            mm(ps[:, 5, 0:D + 2], ones[:, :], rows[:, 3 * (D + 2):4 * (D + 2)], start=True, stop=True).then_inc(S["c_bias_ps"], 1)
            pe.wait_ge(S["c_bias"], 3)

            def graph(b, more):
                def transpose_tile(layer, t):
                    pe.wait_ge(S["xcur"], b * 4 * NT + (layer - 1) * NT + t + 1)
                    n = (layer - 1) * NT + t
                    if n >= 2:
                        pe.wait_ge(S["xt"], b * 3 * NT + n - 1)
                    nc.tensor.transpose(t_bank[t % 2][:, 0:P], xc[:, t, :], ident[:, :]).then_inc(S["xt_ps"], 1)

                def project(layer, t):
                    pe.wait_ge(S["xt"], b * 3 * NT + (layer - 1) * NT + t + 1)
                    width = D + 2 if layer < 3 else D
                    if t >= 2:
                        if layer == 2:
                            pe.wait_ge(S["g2"], b * NT + t - 1)
                        else:
                            pe.wait_ge(S["hb"], b * 2 * NT + (layer // 3) * NT + t - 1)
                    mm(p_bank[t % 2][:, 0:width], x_t[:, t * P:(t + 1) * P], w_x[:, layer - 1, 0:width],
                       start=True, stop=True).then_inc(S["h_ps"], 1)

                def max_bank(n):
                    i, m = n // MAXB, n % MAXB
                    gi, qh = i // QH, i % QH
                    j, qt, kh = m // (2 * QT), m // 2 % QT, m % 2
                    h, q0 = HG * gi + j, qh * BANK + qt * P
                    last = MX_LAST[n]
                    if last >= 0:
                        pe.wait_ge(S["mx" if last % 2 else "over"], b * PAIRS + last // 2 + 1)
                    k0 = (N, BANK)[kh]
                    mm(pre_bank[MX_BANK[n]], qs[0:MROW, h, q0:q0 + P], ks[0:MROW, h, k0:k0 + BANK],
                       start=True, stop=True).then_inc(S["mx_ps"], 1)

                def value_products(u):
                    i, kt, pr = u // UN, u % UN // (HG // HP), u % (HG // HP)
                    if u % UN == 0 and i > 0:
                        pe.wait_ge(S["ot"], b * GRP + i)
                    if kt in POOL_KT[i]:
                        pe.wait_ge(S["p_pool"], b * ALL_P + weighed(POOL_KT, i, kt) + pr + 1)
                    else:
                        pe.wait_ge(S["p_dve"], b * ALL_D + weighed(DVE_KT, i, kt) + pr + 1)
                    for k in range(HP):
                        j = pr * HP + k
                        last = mm(o_bank[SLOT * j:SLOT * (j + 1), :], vaug[:, kt, HG * (i // QH) + j, :],
                                  ring[:, u % RING, k * BANK:(k + 1) * BANK],
                                  start=(kt == 0), stop=(kt == NT - 1), tile_position=(0, SLOT * j), skip_group_check=True)
                    last.then_inc(S["pv"], 1)

                def output_transposes(i):
                    pe.wait_ge(S["ot"], b * GRP + i + 1)
                    if i + 1 < GRP:
                        pe.wait_ge(S["mrow"], b * GRP + i + 1)
                    for t in range(QT):
                        last = nc.tensor.transpose(m_bank[:, t * P:(t + 1) * P], o_t[:, t * P:(t + 1) * P], ident[:, :])
                    last.then_inc(S["ott_ps"], 1)

                def max_rows(i):
                    pe.wait_ge(S["mpart"], b * GRP + i + 1)
                    if i == 0:
                        pe.wait_ge(S["at"], b * NT + NT - 1)
                    if i > 1:
                        pe.wait_ge(S["on"], b * GRP + i - 1)
                    for j in range(HG):
                        for qt in range(QT):
                            last = mm(m_bank[SLOT * j:SLOT * j + 2, qt * P:(qt + 1) * P], mpart[:, j * QT + qt, :],
                                      identb[:, :], start=(qt == 0), stop=(qt == QT - 1), skip_group_check=True,
                                      tile_position=(0, SLOT * j))
                    last.then_inc(S["mrow_ps"], 1)

                def row_transposes(half):
                    pe.wait_ge(S["on"], b * GRP + GRP - 1 + half)
                    if half == 0:
                        pe.wait_ge(S["mx"], (b + 1) * PAIRS)
                    for t in range(QT):
                        last = nc.tensor.transpose(ps[:, (3, 6)[half], t * P:(t + 1) * P], y[:, half * QT + t, :], ident[:, :])
                    last.then_inc(S["ont_ps"], 1)

                def output_projection(half):
                    pe.wait_ge(S["ont"], b * 2 + half + 1)
                    for t in range(half * QT, (half + 1) * QT):
                        last = mm(d4_t[:, t, :], on_t[t], w_t[:, 3, :], start=True, stop=True)
                    last.then_inc(S["wo"], 1)

                pe.wait_ge(S["v_sb"], b + 1)
                for t in range(NT):
                    pe.wait_ge(d_a[t], b * 16 + 16)
                    if t >= 2:
                        pe.wait_ge(S["at"], b * NT + t - 1)
                    for k in range(NT):
                        last = nc.tensor.transpose(at_t[t % 2][:, k, :], a_nat[:, t, k * P:(k + 1) * P], ident[:, :])
                        if k == 3 and t > 0:
                            max_bank(pre_maxima(t)[0])
                            max_bank(pre_maxima(t)[0] + 1)
                    last.then_inc(S["at_ps"], 1)
                    if t == 0:
                        pe.wait_ge(S["d_stack"], b * 16 * 2 * NPROD + 16 * 2 * NPROD)
                    if t == NT - 1:
                        max_rows(0)
                    for n in pre_maxima(t)[min(t, 1):]:
                        max_bank(n)
                        max_bank(n + 1)
                pe.wait_ge(S["at"], b * NT + NT)
                pe.wait_ge(S["mx"], b * PAIRS + PRE // 2)
                for i in range(GRP):
                    gi, qh = i // QH, i % QH
                    pe.wait_ge(S["mrow"], b * GRP + i + 1)
                    for s in range(UN):
                        u = i * UN + s
                        kt, pr = s // (HG // HP), s % (HG // HP)
                        for k in range(HP):
                            h, n = HG * gi + HP * pr + k, HP * u + k
                            if n >= 3:
                                pe.wait_ge(S["p_exp"], b * GRP * UN * HP + n - 2)
                            mm(s_bank[n % 3], ks[:, h, kt * P:(kt + 1) * P],
                               qs[:, h, qh * BANK:(qh + 1) * BANK], start=True, stop=True).then_inc(S["s_ps"], 1)
                        n = PRE + 2 * u
                        if n < GRP * MAXB:
                            max_bank(n)
                        if u >= LAG:
                            value_products(u - LAG)
                        if n < GRP * MAXB:
                            max_bank(n + 1)
                        if s == 9 and i > 0:
                            output_transposes(i - 1)
                        if s == UN - AHEAD // 2 + 1 and i + 1 < GRP:
                            max_rows(i + 1)
                        if s == 12 and i + 1 == GRP:
                            row_transposes(0)
                        if s == 14 and i + 1 == GRP:
                            output_projection(0)
                for u in range(GRP * UN - LAG, GRP * UN):
                    value_products(u)
                output_transposes(GRP - 1)

                pe.wait_ge(S["p_exp"], (b + 1) * GRP * UN * HP)
                transpose_tile(1, 0)
                transpose_tile(1, 1)
                project(1, 0)
                row_transposes(1)
                output_projection(1)
                project(1, 1)
                for s in range(2, NT + 1):
                    if s < NT:
                        transpose_tile(1, s)
                    if s >= 3:
                        project(1, s - 1)

                def graph_product(t, rhs, ready, width, done, free, before):
                    if t >= 2:
                        pe.wait_ge(free, before + t - 1)
                    for k in range(NT):
                        if t == 0:
                            pe.wait_ge(ready, b * NT + k + 1)
                        last = mm(mm_bank[t % 2][:, 0:width], a_t[:, k, t * P:(t + 1) * P], rhs[:, k, 0:width],
                                  start=(k == 0), stop=(k == NT - 1))
                    last.then_inc(done, 1)

                def aj_row(t):
                    pe.wait_ge(S["ext"], b * 2 * NT + NT + t + 1)
                    return mm(d4_t[:, t, :], ext[:, t, 1:2].to_broadcast([P, P]), ident[:, :], start=True, stop=True)

                for s in range(NT + 5):
                    if s < NT:
                        graph_product(s, g, S["g1"], D + 2, S["mm1"], S["y"], b * 4 * NT + NT)
                    if 0 <= s - 3 < NT:
                        transpose_tile(2, s - 3)
                    if 0 <= s - 4 < NT:
                        project(2, s - 4)
                    if s >= 5:
                        last = aj_row(s - 5)
                last.then_inc(S["ajrow_ps"], 1)

                pe.wait_ge(S["g2"], b * NT + NT)
                if more:
                    pe.wait_ge(S["y"], b * 4 * NT + 2 * NT)
                    prepare(b + 1)
                    pe.wait_ge(S["v_sb"], b + 2)

                pe.wait_ge(S["w12"], b + 1)
                for k in range(2):
                    for t in range(NT):
                        last = mm((d2_t, d0_t)[k][:, t, :], w12[:, 1 - k, t:t + 1].to_broadcast([P, P]), ident[:, :], start=True, stop=True)
                    last.then_inc(S["wrow_ps"], 1)
                for k in range(NT):
                    pe.wait_ge(S["p2"], b * NT + k + 1)
                    for t in range(NT):
                        last = mm(mm_bank[t // 3][:, (t % 3) * (D + 1):(t % 3 + 1) * (D + 1)],
                                  ring[:, k, t * P:(t + 1) * P], g2[:, k, 0:D + 1],
                                  start=(k == 0 and t % 3 == 0), stop=(k == NT - 1), skip_group_check=True)
                last.then_inc(S["mm2"], 1)
                for s in range(NT + 1):
                    if s < NT:
                        transpose_tile(3, s)
                    if s >= 1:
                        project(3, s - 1)

                for t in range(NT):
                    graph_product(t, g, S["g3"], D, S["mm3"], S["mm3_free"], b * NT)
                pe.wait_ge(S["mm3_free"], b * NT + NT)

            with pe.Fori(0, B - 1) as b:
                graph(b, True)
            graph(B - 1, False)


_INS = ['x', 'adj', 'nodemask', 'L0_gnn_Wq', 'L0_gnn_Wk', 'L0_gnn_Wv', 'L0_gnn_Wo', 'L0_gnn_bo',
        'L1_gnn_W_w', 'L1_gnn_W_b', 'L1_gnn_a_w', 'L1_gnn_a_b', 'L2_gnn_W', 'L2_gnn_bW', 'L2_gnn_wai',
        'L2_gnn_bai', 'L2_gnn_waj', 'L2_gnn_baj', 'L3_gnn_W', 'L3_gnn_b']


def kernel(**inputs):
    import numpy as _np
    import concourse.bacc as _bacc
    from concourse import mybir as _mybir
    from concourse.bass_utils import run_bass_kernel_spmd as _run

    nc = _bacc.Bacc("TRN2", target_bir_lowering=False, num_devices=1)
    arrays, args = {}, []
    for name in _INS:
        a = _np.ascontiguousarray(inputs[name])
        arrays[f"in_{name}_dram"] = a
        args.append(nc.dram_tensor(f"in_{name}_dram", a.shape, _mybir.dt.from_np(a.dtype), kind="ExternalInput").ap())
    out = nc.dram_tensor("out_0_dram", inputs['x'].shape, _mybir.dt.from_np(_np.dtype('float32')), kind="ExternalOutput").ap()
    gnn_stack_kernel(nc, *args, out)
    r = _run(nc, [arrays], core_ids=[0])
    return r.results[0]["out_0_dram"]
```
